# Optimizing a Trainium2 kernel written in Bass

```python
import numpy as np
import jax
import jax.numpy as jnp

def _softmax(x, axis=-1):
    return jax.nn.softmax(x, axis=axis)

def _gelu(x):
    return jax.nn.gelu(x, approximate=True)

def _silu(x):
    return jax.nn.silu(x)

def _sigmoid(x):
    return jax.nn.sigmoid(x)

def _layernorm(x, axis=-1, eps=1e-05):
    m = jnp.mean(x, axis=axis, keepdims=True)
    v = jnp.var(x, axis=axis, keepdims=True)
    return (x - m) / jnp.sqrt(v + eps)

def _scatter_add(tgt, idx, src, axis=0):
    return tgt.at[idx].add(src)

def _segment_sum(src, seg, n):
    return jax.ops.segment_sum(src, seg, n)
kernel_name = 'mk_gnn_preln_d2_gnn_r8_4da9fe'

def setup_inputs(seed: int=0):
    np.random.seed(seed)
    _w = jnp.asarray

    def _rec_inputs():
        import jax
        import jax.numpy as jnp
        _gk = jax.random.key(seed)
        x = -0.0003713 + 1 * jax.random.normal(jax.random.fold_in(_gk, 1), (6250, 128), jnp.float32)
        _s = jax.random.randint(jax.random.fold_in(_gk, 2), (100000,), 0, 6250, jnp.int32)
        _d = jax.random.randint(jax.random.fold_in(_gk, 3), (100000,), 0, 6250, jnp.int32)
        _loop = jnp.arange(6250, dtype=jnp.int32)
        src = jnp.concatenate([_s, _d, _loop])
        dst = jnp.concatenate([_d, _s, _loop])
        _o = jnp.argsort(dst, stable=True)
        src = src[_o]
        dst = dst[_o]
        edge_attr_128 = -6.47781e-05 + 0.999943 * jax.random.normal(jax.random.fold_in(_gk, 12), (206250, 128), jnp.float32)
        return (x, src, dst, edge_attr_128)
    x, src, dst, edge_attr_128 = _rec_inputs()

    def _L0_gnn_setup():
        import jax, jax.numpy as jnp
        import numpy as np
        N_NODES = 12500
        N_EDGES = 200000
        N_NODE_F = 128
        N_EDGE_F = 128
        N_GLOBAL_F = 64
        N_GRAPHS = 256
        HIDDEN = 128
        IN_DIM = N_NODE_F + N_EDGE_F + N_GLOBAL_F
        key = jax.random.key(seed)
        k1, k2, k3, k4, k5, k6 = jax.random.split(key, 6)
        node_feats = jax.random.normal(k1, (N_NODES, N_NODE_F), dtype=jnp.float32)
        edge_feats = jax.random.normal(k2, (N_EDGES, N_EDGE_F), dtype=jnp.float32)
        global_feats = jax.random.normal(k3, (N_GRAPHS, N_GLOBAL_F), dtype=jnp.float32)
        W = jax.random.normal(k4, (HIDDEN, IN_DIM), dtype=jnp.float32) * (1.0 / np.sqrt(IN_DIM))
        edge_index = jax.random.randint(k5, (2, N_EDGES), 0, N_NODES, dtype=jnp.int64)
        batch = jnp.sort(jax.random.randint(k6, (N_NODES,), 0, N_GRAPHS, dtype=jnp.int64))
        return {'node_feats': node_feats, 'edge_feats': edge_feats, 'global_feats': global_feats, 'W': W, 'edge_index': edge_index, 'batch': batch}
    _L0_gnn_all = _L0_gnn_setup()
    _L0_gnn_in = {k: v for k, v in _L0_gnn_all.items() if k in ('global_feats', 'W')}
    del _L0_gnn_all

    def _L1_gnn_setup():
        import jax, jax.numpy as jnp
        import numpy as np
        N_NODES = 12500
        N_EDGES = 75000
        DIM = 128
        key = jax.random.key(seed)
        ks = jax.random.split(key, 7)
        scale = 1.0 / np.sqrt(DIM)
        h = jax.random.normal(ks[0], (N_NODES, DIM), dtype=jnp.float32)
        edges = jax.random.randint(ks[1], (2, N_EDGES), 0, N_NODES, dtype=jnp.int32)
        Wq = jax.random.normal(ks[2], (DIM, DIM), dtype=jnp.float32) * scale
        Wk = jax.random.normal(ks[3], (DIM, DIM), dtype=jnp.float32) * scale
        Wv = jax.random.normal(ks[4], (DIM, DIM), dtype=jnp.float32) * scale
        Wp = jax.random.normal(ks[5], (DIM, DIM), dtype=jnp.float32) * scale
        bp = jnp.zeros((DIM,), dtype=jnp.float32)
        return {'h': h, 'edges': edges, 'Wq': Wq, 'Wk': Wk, 'Wv': Wv, 'Wp': Wp, 'bp': bp}
    _L1_gnn_all = _L1_gnn_setup()
    _L1_gnn_in = {k: v for k, v in _L1_gnn_all.items() if k in ('Wq', 'Wk', 'Wv', 'Wp', 'bp')}
    del _L1_gnn_all
    return {'x': x, 'src': src, 'dst': dst, 'edge_attr_128': edge_attr_128, 'L0_gnn_global_feats': _L0_gnn_in['global_feats'], 'L0_gnn_W': _L0_gnn_in['W'], 'L1_gnn_Wq': _L1_gnn_in['Wq'], 'L1_gnn_Wk': _L1_gnn_in['Wk'], 'L1_gnn_Wv': _L1_gnn_in['Wv'], 'L1_gnn_Wp': _L1_gnn_in['Wp'], 'L1_gnn_bp': _L1_gnn_in['bp']}

def reference(x, src, dst, edge_attr_128, L0_gnn_global_feats, L0_gnn_W, L1_gnn_Wq, L1_gnn_Wk, L1_gnn_Wv, L1_gnn_Wp, L1_gnn_bp):
    import jax
    import jax.numpy as jnp

    def _L0_gnn_ref(node_feats, edge_feats, global_feats, W, edge_index, batch):
        import jax, jax.numpy as jnp
        import numpy as np
        N_NODES = 12500
        N_EDGES = 200000
        N_NODE_F = 128
        N_EDGE_F = 128
        N_GLOBAL_F = 64
        N_GRAPHS = 256
        HIDDEN = 128
        IN_DIM = N_NODE_F + N_EDGE_F + N_GLOBAL_F
        n_nodes = node_feats.shape[0]
        idx_dst = edge_index[1]
        sums = jax.ops.segment_sum(edge_feats, idx_dst, num_segments=n_nodes)
        counts = jax.ops.segment_sum(jnp.ones((edge_feats.shape[0],), dtype=edge_feats.dtype), idx_dst, num_segments=n_nodes)
        mean_edge = sums / jnp.maximum(counts, 1.0)[:, None]
        out = jnp.concatenate([node_feats, mean_edge, global_feats[batch]], axis=1)
        h = jnp.einsum('ni,oi->no', out, W)
        return jax.nn.softplus(h) - jnp.log(jnp.asarray(2.0, dtype=h.dtype))

    def _L1_gnn_ref(h, edges, Wq, Wk, Wv, Wp, bp):
        import jax, jax.numpy as jnp
        import numpy as np
        N_NODES = 12500
        N_EDGES = 75000
        DIM = 128
        src, dst = (edges[0], edges[1])
        N, d = h.shape
        q = h @ Wq.T
        k = h @ Wk.T
        v = h @ Wv.T
        scores = jnp.sum(q[dst] * k[src], axis=1) / jnp.sqrt(jnp.asarray(d, h.dtype))
        max_per_dst = jax.ops.segment_max(scores, dst, num_segments=N)
        exp = jnp.exp(jnp.clip(scores - max_per_dst[dst], -50.0, 50.0))
        sum_per_dst = jax.ops.segment_sum(exp, dst, num_segments=N)
        alpha = exp / (sum_per_dst[dst] + 1e-09)
        alpha = jnp.nan_to_num(alpha, nan=0.0, posinf=0.0, neginf=0.0)
        agg = jax.ops.segment_sum(v[src] * alpha[:, None], dst, num_segments=N)
        return jax.nn.relu(agg @ Wp.T + bp + h)
    edge_index = jnp.stack([src, dst])
    batch0 = jnp.zeros((6250,), jnp.int32)
    h = jnp.maximum(_layernorm(x, axis=-1), 0.0)
    x = x + _L0_gnn_ref(h, edge_attr_128, L0_gnn_global_feats, L0_gnn_W, edge_index, batch0)
    h = jnp.maximum(_layernorm(x, axis=-1), 0.0)
    x = x + _L1_gnn_ref(h, edge_index, L1_gnn_Wq, L1_gnn_Wk, L1_gnn_Wv, L1_gnn_Wp, L1_gnn_bp)
    return x

_drawn_inputs = setup_inputs


def setup_inputs(seed=0):
    import zlib

    import numpy as np

    out = dict(_drawn_inputs(seed))
    spreads = {'L1_gnn_bp': (0.0, 0.1)}
    factors = {}
    for name, (base, spread) in spreads.items():
        noise = np.random.default_rng([zlib.crc32(name.encode()), seed]).standard_normal(out[name].shape)
        drawn = base * np.exp(spread * noise) if base else spread * noise
        out[name] = jnp.asarray(drawn.astype(out[name].dtype))
    for name, factor in factors.items():
        out[name] = (out[name] * factor).astype(out[name].dtype)
    return out
```

```python
from contextlib import ExitStack

import concourse.bass as bass
from concourse import mybir

F32 = mybir.dt.float32
BF16 = mybir.dt.bfloat16
I32 = mybir.dt.int32
ALU = mybir.AluOpType
ACT = mybir.ActivationFunctionType
AX = mybir.AxisListType

P = 128
J = 13
GROUP = P * J
W = 64
NT = 125
CT = 5
RING = 4
BIG = 1.0e30
CLIP = 1.9287498479639178e-22
LN_EPS = 1e-5
LN_STEPS = 9
LN2 = 0.6931471805599453


def build(nc, x, src, dst, edge_attr, global_feats, W0, Wq, Wk, Wv, Wp, bp, out):
    N, D = x.shape
    E = src.shape[0]
    GF = global_feats.shape[1]
    assert D == P and N % (NT * CT) == 0
    G = -(-E // GROUP)
    LAST = E - GROUP
    REPEATED = (G - 1) * GROUP - LAST
    assert G % RING == 0 and G % 2 == 0 and 0 <= REPEATED < GROUP and G <= P
    TILES = N // NT
    CHUNKS = TILES // CT
    CN = CT * NT
    NW = -(-N // W)
    NPAD = N + W
    SCALE = float(D) ** -0.5

    x_t = x.rearrange("(t p) d -> p t d", p=NT)
    out_t = out.rearrange("(t p) d -> p t d", p=NT)

    def group_edges(g):
        return edge_attr[bass.ds(g * GROUP, GROUP), :].rearrange("(p j) d -> p j d", j=J)

    def group_sources(g):
        return src[bass.ds(g * GROUP, GROUP)].rearrange("(p j) -> p j", j=J)

    with ExitStack() as ctx:
        def sb(name, shape, dt=F32):
            return ctx.enter_context(nc.sbuf_tensor(name, shape, dt))

        def ps(name, shape, dt=F32):
            return ctx.enter_context(nc.psum_tensor(name, shape, dt))

        def sem(name):
            return ctx.enter_context(nc.semaphore(name))

        h_table = nc.dram_tensor("h_table", [N, D], F32, kind="Internal").ap()
        h_table_t = h_table.rearrange("(t p) d -> p t d", p=NT)

        ident = sb("ident", [P, P])
        ones = sb("ones", [P, P])
        ones16 = sb("ones16", [P, P], BF16)
        window_iota = sb("window_iota", [P, W])
        W0_sb = sb("W0_sb", [P, 2 * D + GF])
        WnT = sb("WnT", [P, P])
        WeT = sb("WeT", [P, P])
        WgT = sb("WgT", [GF, P])
        Wq_sb = sb("Wq_sb", [P, P])
        Wk_sb = sb("Wk_sb", [P, P])
        Wv_sb = sb("Wv_sb", [P, P])
        Wp_sb = sb("Wp_sb", [P, P])
        WpT = sb("WpT", [P, P])
        Wqk = sb("Wqk", [P, P])
        Wvp = sb("Wvp", [P, P])
        g0 = sb("g0", [GF, 1])
        g0_rep = sb("g0_rep", [GF, NT])
        bp_row = sb("bp_row", [1, P])

        dst_f = sb("dst_f", [P, G * J])
        dst_w = sb("dst_w", [P, G * J])
        wide_f = dst_f[:, :]
        rel = sb("rel", [P, J])
        low_p = sb("low_p", [P, G])
        high_p = sb("high_p", [P, G])
        low = sb("low", [G, 1])
        high = sb("high", [G, 1])
        low_diag = sb("low_diag", [G, G])
        base_i = sb("base_i", [1, G], I32)
        span_row = sb("span_row", [1, G])
        widest = sb("widest", [1, 1])
        wide_i = sb("wide_i", [1, 1], I32)

        X = sb("X", [NT, TILES, D])
        acc = sb("acc", [P, NPAD])
        norm = sb("norm", [P, NPAD])
        top = sb("top", [P, NPAD])
        QK = sb("QK", [P, NPAD])

        dst_i = QK[:, 0:G * J].bitcast(I32)

        rows = sb("rows", [P, RING, J, D])
        onehot = sb("onehot", [P, 2, J, W])
        onehot16 = sb("onehot16", [P, 2, J, W], BF16)

        srcs = sb("srcs", [P, RING, J], I32)
        rowsT = sb("rowsT", [P, J, P])
        unmask = onehot16[:, :, :, :].rearrange("p s j n -> p (s j n)").bitcast(F32) \
            .rearrange("p (j n) -> p j n", n=W)
        masked = sb("masked", [P, J, W])
        centred = sb("centred", [P, J, W])
        probs = sb("probs", [P, J, W])
        tile_top = sb("tile_top", [P, P])
        group_top = sb("group_top", [W, 1])
        top_diag = sb("top_diag", [W, W])
        new_top = sb("new_top", [P, W])
        drop = sb("drop", [P, W])
        rescale = sb("rescale", [P, 2, W])

        def ln_tiles(name, n):
            return [sb(f"{name}_stats", [NT, n, 6])] + \
                [sb(f"{name}_{what}", [NT, n]) for what in ("mean2", "diff", "var", "rstd", "shift")]

        ln1 = ln_tiles("ln1", TILES)
        ln2 = ln_tiles("ln2", CT)
        var, rstd, shift = ln1[3:]
        var2, rstd2, shift2 = ln2[3:]

        def chunk_buffer(slot, half, parts=P):
            return rows[0:parts, slot].rearrange("p j d -> p (j d)")[:, half * 6 * D:half * 6 * D + CT * D]\
                .rearrange("p (t d) -> p t d", d=D)

        h1 = chunk_buffer(0, 0, NT)
        h1T = chunk_buffer(0, 1)
        meanT = chunk_buffer(1, 0)
        softp = chunk_buffer(1, 1, NT)
        h2 = chunk_buffer(2, 0, NT)
        h2T_flat = chunk_buffer(2, 1).rearrange("p t d -> p (t d)")[:, 0:CN]
        aggT = [chunk_buffer(0, 0), chunk_buffer(0, 1)]
        h_in = [chunk_buffer(1, 0, NT), chunk_buffer(1, 1, NT)]
        y = [chunk_buffer(2, 0, NT), chunk_buffer(2, 1, NT)]

        pA = ps("pA", [P, 2, 512])
        pB = ps("pB", [P, 2, 512])
        pC = ps("pC", [P, 2, 512])
        pD = ps("pD", [P, 2, 512])

        def two_banks(t):
            return t[:, :, :].rearrange("p b n -> p (b n)")

        def node_tiles(t, width=P):
            return two_banks(t)[:, 0:CT * P].rearrange("p (t d) -> p t d", d=P)[:, :, 0:width]

        scores_ps = [two_banks(t)[:, 0:J * W].rearrange("p (j n) -> p j n", n=W) for t in (pB, pC)]
        turned_ps = pD[:, 0, 0:P]
        spread_ps = pD[:, 0, P:P + W]
        agg_ps = pD[:, 1, 0:W]
        sum_ps = pD[:, 1, W:2 * W]

        dst_loaded = sem("dst_loaded")
        x_loaded = sem("x_loaded")
        weights_loaded = sem("weights_loaded")
        edges_loaded = [sem(f"edges_loaded{i}") for i in range(RING)]
        const_made = sem("const_made")
        zeroed = sem("zeroed")
        weight_turned = sem("weight_turned")
        weight_copied = sem("weight_copied")
        prep = sem("prep")
        bounds_turned = sem("bounds_turned")
        repeated_masked = sem("repeated_masked")
        base_ready = sem("base_ready")

        onehot_ready = sem("onehot_ready")
        onehot16_ready = sem("onehot16_ready")
        sums_ready = sem("sums_ready")
        counts_ready = sem("counts_ready")
        sums_added = sem("sums_added")
        counts_added = sem("counts_added")
        wide_step = sem("wide_step")

        ln_step = sem("ln_step")
        stats_ready = sem("stats_ready")
        var_ready = sem("var_ready")
        log_ready = sem("log_ready")
        root_ready = sem("root_ready")
        inverse_ready = sem("inverse_ready")
        h1_ready = sem("h1_ready")
        h1_turned = sem("h1_turned")
        h1T_ready = sem("h1T_ready")
        meanT_ready = sem("meanT_ready")
        update_ready = sem("update_ready")
        softp_step = sem("softp_step")
        softp_ready = sem("softp_ready")
        softp_summed = sem("softp_summed")
        x1_ready = sem("x1_ready")
        ln2_ready = sem("ln2_ready")
        h2_turn = sem("h2_turn")
        h2_ready = sem("h2_ready")
        h2_stored = sem("h2_stored")
        h2_turned = sem("h2_turned")
        h2T_ready = sem("h2T_ready")
        qk_ready = sem("qk_ready")
        qk_stored = sem("qk_stored")

        cleared = sem("cleared")
        qk_padded = sem("qk_padded")
        srcs_loaded = [sem(f"srcs_loaded{i}") for i in range(RING)]
        gather_turn = sem("gather_turn")
        gathered = [sem(f"gathered{i}") for i in range(RING)]
        rows_turned = sem("rows_turned")
        rowsT_ready = sem("rowsT_ready")
        scores_ready = sem("scores_ready")
        hot_ready = sem("hot_ready")
        unmask_ready = sem("unmask_ready")
        masked_ready = sem("masked_ready")
        tile_top_ready = sem("tile_top_ready")
        top_turned = sem("top_turned")
        group_top_ready = sem("group_top_ready")
        top_diag_ready = sem("top_diag_ready")
        top_spread = sem("top_spread")
        new_top_ready = sem("new_top_ready")
        drop_ready = sem("drop_ready")
        rescale_ready = sem("rescale_ready")
        top_stored = sem("top_stored")
        centred_ready = sem("centred_ready")
        exp_ready = sem("exp_ready")
        probs_ready = sem("probs_ready")
        agg_ready = sem("agg_ready")
        scaled = sem("scaled")
        agg_added = sem("agg_added")
        wide2_step = sem("wide2_step")

        sum_inverted = sem("sum_inverted")
        aggT_ready = sem("aggT_ready")
        h_in_loaded = [sem(f"h_in_loaded{i}") for i in range(2)]
        out_mm = sem("out_mm")
        y_step = sem("y_step")
        y_ready = sem("y_ready")
        out_stored = [sem(f"out_stored{i}") for i in range(2)]

        GATHER = 16 * J
        WIDE = G

        def wait_if(eng, s, value):
            if not isinstance(value, int) or value > 0:
                eng.wait_ge(s, value)

        def over_tiles(row, n=W):
            return row.unsqueeze(1).to_broadcast([P, J, n])

        def over_window(cols):
            return cols.unsqueeze(2).to_broadcast([P, J, W])

        def load_base(eng, g):
            return eng.value_load(base_i[0:1, bass.ds(g, 1)], min_val=0, max_val=N - 1)

        def load_wide(eng):
            return eng.value_load(wide_i[0:1, 0:1], min_val=0, max_val=1)

        block = ctx.enter_context(nc.Block())

        @block.sync
        def _(sp):
            sp.dma_start(dst_i[:, 0:(G - 1) * J].rearrange("p (g j) -> p g j", j=J),
                         dst[0:(G - 1) * GROUP].rearrange("(g p j) -> p g j", p=P, j=J)).then_inc(dst_loaded, 16)
            sp.dma_start(dst_i[:, (G - 1) * J:G * J],
                         dst[LAST:E].rearrange("(p j) -> p j", j=J)).then_inc(dst_loaded, 16)
            for tile, source in ((W0_sb, W0), (Wq_sb, Wq), (Wk_sb, Wk), (Wv_sb, Wv), (Wp_sb, Wp)):
                sp.dma_start(tile[:, :], source).then_inc(weights_loaded, 16)
            sp.dma_start(bp_row[:, :], bp.unsqueeze(0)).then_inc(weights_loaded, 16)
            sp.dma_start(g0[:, :], global_feats[0:1, :].rearrange("a f -> f a")).then_inc(weights_loaded, 16)
            sp.dma_start(X[:, :, :], x_t).then_inc(x_loaded, 16)

            def load_edges(source, slot, free):
                wait_if(sp, sums_ready, free)
                sp.dma_start(rows[:, slot], source).then_inc(edges_loaded[slot], 16)

            for g in range(RING):
                load_edges(group_edges(g), g, 0)
            with sp.Fori(1, G // RING - 1) as k:
                for i in range(RING):
                    load_edges(group_edges(k * RING + i), i, k * RING + (i - RING + 1))
            for g in range(G - RING, G - 1):
                load_edges(group_edges(g), g % RING, g - RING + 1)
            last_edges = edge_attr[LAST:E, :].rearrange("(p j) d -> p j d", j=J)
            load_edges(last_edges, (G - 1) % RING, G - RING)

            sp.wait_ge(base_ready, 1)
            wide = load_wide(sp)
            with sp.If(wide > 0):
                with sp.Fori(0, G - 1) as g:
                    load_edges(group_edges(g), 0, WIDE + g * NW)
                load_edges(last_edges, 0, WIDE + (G - 1) * NW)

            with sp.Fori(0, CHUNKS) as c:
                sp.wait_ge(h2_ready, c + 1)
                sp.dma_start(h_table_t[:, bass.ds(c * CT, CT), :], h2).then_inc(h2_stored, 16)

            def load_sources(source, slot, engine_done):
                for s, value in engine_done:
                    wait_if(sp, s, value)
                sp.dma_start(srcs[:, slot], source).then_inc(srcs_loaded[slot], 16)

            for g in range(RING):
                load_sources(group_sources(g), g, [])
            with sp.Fori(1, G // RING - 1) as k:
                for i in range(RING):
                    load_sources(group_sources(k * RING + i), i, [(gathered[i], k * GATHER)])
            for g in range(G - RING, G - 1):
                load_sources(group_sources(g), g % RING, [(gathered[g % RING], g // RING * GATHER)])
            last_sources = src[LAST:E].rearrange("(p j) -> p j", j=J)
            load_sources(last_sources, (G - 1) % RING, [(gathered[(G - 1) % RING], (G // RING - 1) * GATHER)])
            with sp.If(wide > 0):
                with sp.Fori(0, G - 1) as g:
                    load_sources(group_sources(g), 0, [(gathered[0], (g + G // RING) * GATHER)])
                load_sources(last_sources, 0, [(gathered[0], (G - 1 + G // RING) * GATHER)])

            def load_h(c, slot):
                sp.dma_start(h_in[slot], h_table_t[:, bass.ds(c * CT, CT), :]).then_inc(h_in_loaded[slot], 16)

            def store_y(c, slot):
                sp.wait_ge(y_ready, c + 1)
                sp.dma_start(out_t[:, bass.ds(c * CT, CT), :], y[slot]).then_inc(out_stored[slot], 16)

            sp.wait_ge(sum_inverted, 2)
            load_h(0, 0)
            load_h(1, 1)
            with sp.Fori(0, CHUNKS // 2 - 1) as k:
                for i in range(2):
                    store_y(k * 2 + i, i)
                    load_h(k * 2 + i + 2, i)
            for i in range(2):
                store_y(CHUNKS - 2 + i, i)
            for i in range(2):
                sp.wait_ge(out_stored[i], 16 * (CHUNKS // 2))

        @block.gpsimd
        def _(pool):
            pool.memset(ident[:, :], 0.0).then_inc(const_made, 1)
            pool.memset(ones[:, :], 1.0).then_inc(const_made, 1)
            pool.memset(ones16[:, :], 1.0).then_inc(const_made, 1)
            pool.memset(tile_top[:, :], 0.0).then_inc(const_made, 1)
            pool.iota(window_iota[:, :], pattern=[[1, W]], base=0, channel_multiplier=0,
                      allow_small_or_imprecise_dtypes=True).then_inc(const_made, 1)
            pool.wait_ge(const_made, 5)
            pool.affine_select(out=ident[:, :], in_=ident[:, :], compare_op=ALU.not_equal, fill=1.0, base=0,
                               pattern=[[-1, P]], channel_multiplier=1).then_inc(const_made, 1)
            pool.memset(acc[:, :], 0.0).then_inc(zeroed, 1)
            pool.memset(norm[:, :], 0.0).then_inc(zeroed, 1)
            pool.wait_ge(prep, 3)
            pool.affine_select(out=dst_f[:, (G - 1) * J:G * J], in_=dst_f[:, (G - 1) * J:G * J],
                               compare_op=ALU.is_ge, fill=-1.0, base=-REPEATED, pattern=[[1, J]],
                               channel_multiplier=J).then_inc(repeated_masked, 1)
            pool.memset(top[:, :], -BIG).then_inc(cleared, 1)
            pool.memset(QK[:, N:NPAD], 0.0).then_inc(qk_padded, 1)

            pool.wait_ge(meanT_ready, CHUNKS)
            pool.memset(acc[:, :], 0.0).then_inc(cleared, 1)
            pool.memset(norm[:, :], 0.0).then_inc(cleared, 1)

            last_row = pool.to_reg(N - 1)

            def gather(slot, loads, free):
                pool.wait_ge(srcs_loaded[slot], loads)
                wait_if(pool, agg_ready, free)
                pool.sem_inc(gather_turn, 1)
                for j in range(J):
                    pool.indirect_dma_start(
                        out=rows[:, slot, j, :], out_offset=None, in_=h_table,
                        in_offset=bass.IndirectOffsetOnAxis(ap=srcs[:, slot, j:j + 1], axis=0),
                        bounds_check=last_row).then_inc(gathered[slot], 16)

            pool.wait_ge(h2_stored, 16 * CHUNKS)
            pool.wait_ge(qk_ready, CHUNKS)
            pool.wait_ge(x1_ready, CHUNKS)
            for g in range(RING):
                gather(g, 16, 0)
            with pool.Fori(1, G // RING) as k:
                for i in range(RING):
                    gather(i, (k + 1) * 16, k * RING + (i - RING + 1))
            pool.wait_ge(base_ready, 1)
            wide = load_wide(pool)
            with pool.If(wide > 0):
                with pool.Fori(0, G) as g:
                    gather(0, (g + G // RING + 1) * 16, WIDE + g * NW)

        @block.tensor
        def _(pe):
            pe.wait_ge(const_made, 6)
            pe.wait_ge(weights_loaded, 16 * 7)
            pe.transpose(pA[:, 0, 0:P], W0_sb[:, 0:D], ident[:, :])
            pe.transpose(pA[:, 0, P:2 * P], W0_sb[:, D:2 * D], ident[:, :])
            pe.transpose(pA[0:GF, 0, 2 * P:3 * P], W0_sb[:, 2 * D:2 * D + GF], ident[:, :])
            pe.transpose(pA[:, 0, 3 * P:4 * P], Wp_sb[:, :], ident[:, :]).then_inc(weight_turned, 1)
            pe.matmul(pA[:, 1, 0:P], Wq_sb[:, :], Wk_sb[:, :], start=True, stop=True).then_inc(weight_turned, 1)
            pe.wait_ge(weight_copied, 4)
            pe.matmul(pB[:, 0, 0:P], Wv_sb[:, :], WpT[:, :], start=True, stop=True).then_inc(weight_turned, 1)

            pe.wait_ge(prep, 3)
            pe.transpose(pD[0:G, 0, 0:P], low_p[:, :], ident[:, :])
            pe.transpose(pD[0:G, 0, P:2 * P], high_p[:, :], ident[:, :]).then_inc(bounds_turned, 1)
            pe.wait_ge(prep, 6)
            pe.matmul(pD[:, 1, 0:G], ones[0:G, :], low_diag[:, :], start=True, stop=True).then_inc(bounds_turned, 1)
            pe.transpose(pD[0:1, 1, P:P + G], high[:, :], ident[0:G, 0:G]).then_inc(bounds_turned, 1)

            def sums(slot, edge_slot, loads, n, lag):
                pe.wait_ge(edges_loaded[edge_slot], loads)
                pe.wait_ge(onehot_ready, n + 1)
                wait_if(pe, sums_added, n - lag + 1)
                for j in range(J):
                    mm = pe.matmul(pA[:, slot, 0:W], rows[:, edge_slot, j, :], onehot[:, slot, j, :],
                                   start=(j == 0), stop=(j == J - 1))
                mm.then_inc(sums_ready, 1)
                pe.wait_ge(onehot16_ready, n + 1)
                wait_if(pe, counts_added, n - lag + 1)
                for j in range(J):
                    mm = pe.matmul(pB[:, slot, 0:W], ones16[:, :], onehot16[:, slot, j, :],
                                   start=(j == 0), stop=(j == J - 1))
                mm.then_inc(counts_ready, 1)

            pe.wait_ge(weight_copied, 7)
            for g in range(RING):
                sums(g % 2, g, 16, g, 2)
            with pe.Fori(1, G // RING) as k:
                for i in range(RING):
                    sums(i % 2, i, (k + 1) * 16, k * RING + i, 2)
            pe.wait_ge(base_ready, 1)
            wide = load_wide(pe)
            with pe.If(wide > 0):
                with pe.Fori(0, G) as g:
                    with pe.Fori(0, NW) as w:
                        sums(0, 0, (g + G // RING + 1) * 16, g * NW + w + WIDE, 1)

            with pe.Fori(0, CHUNKS) as c:
                pe.wait_ge(h1_ready, c + 1)
                pe.wait_ge(h1T_ready, c)
                for t in range(CT):
                    mm = pe.transpose(node_tiles(pA, NT)[:, t, :], h1[:, t, :], ident[0:NT, 0:NT])
                mm.then_inc(h1_turned, 1)
                pe.wait_ge(h1T_ready, c + 1)
                pe.wait_ge(meanT_ready, c + 1)
                pe.wait_ge(softp_summed, c)
                for t in range(CT):
                    o = node_tiles(pB)[0:NT, t, :]
                    pe.matmul(o, h1T[:, t, 0:NT], WnT[:, :], start=True, stop=False)
                    pe.matmul(o, meanT[:, t, 0:NT], WeT[:, :], start=False, stop=False)
                    mm = pe.matmul(o, g0_rep[:, :], WgT[:, :], start=False, stop=True)
                mm.then_inc(update_ready, 1)
                pe.wait_ge(h2_ready, c + 1)
                pe.wait_ge(h2T_ready, c)
                for t in range(CT):
                    mm = pe.transpose(node_tiles(pC, NT)[:, t, :], h2[:, t, :], ident[0:NT, 0:NT])
                mm.then_inc(h2_turned, 1)
                pe.wait_ge(h2T_ready, c + 1)
                pe.wait_ge(qk_stored, c)
                pe.matmul(pD[:, 0, :], Wqk[:, :], h2T_flat[:, 0:512], start=True, stop=True)
                pe.matmul(pD[:, 1, 0:CN - 512], Wqk[:, :], h2T_flat[:, 512:CN],
                          start=True, stop=True).then_inc(qk_ready, 1)

            pe.wait_ge(qk_stored, CHUNKS)
            pe.wait_ge(qk_padded, 1)
            TURNS = [range(0, 4), range(4, 7), range(7, 10), range(10, 13)]

            def turn_rows(rows_slot, gathers, m):
                pe.wait_ge(gathered[rows_slot], gathers)
                for q, tiles in enumerate(TURNS):
                    wait_if(pe, rowsT_ready, m * 4 + q - 1)
                    for a, j in enumerate(tiles):
                        mm = pe.transpose(pA[:, q % 2, a * P:(a + 1) * P], rows[:, rows_slot, j, :], ident[:, :])
                    mm.then_inc(rows_turned, 1)

            def scores(slot, base, n, m, lag):
                pe.wait_ge(rowsT_ready, m * 4 + 4)
                wait_if(pe, masked_ready, n - lag + 1)
                for j in range(J):
                    mm = pe.matmul(scores_ps[slot][:, j, :], rowsT[:, j, :], QK[:, bass.ds(base, W)],
                                   start=True, stop=True)
                mm.then_inc(scores_ready, 1)

            def spread_top(n):
                pe.wait_ge(tile_top_ready, n + 1)
                wait_if(pe, group_top_ready, n)
                pe.transpose(turned_ps, tile_top[:, :], ident[:, :]).then_inc(top_turned, 1)
                pe.wait_ge(top_diag_ready, n + 1)
                wait_if(pe, new_top_ready, n)
                pe.matmul(spread_ps, ones[0:W, :], top_diag[:, :], start=True, stop=True).then_inc(top_spread, 1)

            def aggregate(rows_slot, n):
                pe.wait_ge(probs_ready, n + 1)
                wait_if(pe, agg_added, 2 * n)
                for j in range(J):
                    pe.matmul(agg_ps, rows[:, rows_slot, j, :], probs[:, j, :],
                              start=(j == 0), stop=(j == J - 1))
                for j in range(J):
                    mm = pe.matmul(sum_ps, ones[:, :], probs[:, j, :], start=(j == 0), stop=(j == J - 1))
                mm.then_inc(agg_ready, 1)

            def first_half(i, g, gathers):
                turn_rows(i, gathers, g)
                scores(i % 2, load_base(pe, g), g, g, 2)

            first_half(0, 0, GATHER)
            spread_top(0)
            for g in range(1, RING):
                first_half(g, g, GATHER)
                aggregate(g - 1, g - 1)
                spread_top(g)
            with pe.Fori(1, G // RING) as k:
                for i in range(RING):
                    g = k * RING + i
                    first_half(i, g, (k + 1) * GATHER)
                    aggregate((i - 1) % RING, g - 1)
                    spread_top(g)
            aggregate((G - 1) % RING, G - 1)
            with pe.If(wide > 0):
                with pe.Fori(0, G) as g:
                    turn_rows(0, (g + G // RING + 1) * GATHER, g + G)
                    with pe.Fori(0, NW) as w:
                        n = g * NW + w + WIDE
                        scores(0, w * W, n, g + G, 1)
                        spread_top(n)
                        aggregate(0, n)

            with pe.Fori(0, CHUNKS // 2) as k:
                for i in range(2):
                    c = k * 2 + i
                    pe.wait_ge(aggT_ready, c + 1)
                    pe.wait_ge(y_step, c)
                    for t in range(CT):
                        o = node_tiles((pB, pC)[i])[0:NT, t, :]
                        pe.matmul(o, aggT[i][:, t, 0:NT], Wvp[:, :], start=True, stop=False)
                        mm = pe.matmul(o, ones[0:1, 0:NT], bp_row[:, :], start=False, stop=True)
                    mm.then_inc(out_mm, 1)

        @block.scalar
        def _(act):
            def onehot_cast(slot, n, lag):
                act.wait_ge(onehot_ready, n + 1)
                wait_if(act, counts_ready, n - lag + 1)
                act.activation(onehot16[:, slot], onehot[:, slot], ACT.Copy).then_inc(onehot16_ready, 1)

            onehot_cast(0, 0, 2)
            onehot_cast(1, 1, 2)
            with act.Fori(1, G // 2) as k:
                for i in range(2):
                    onehot_cast(i, k * 2 + i, 2)
            act.wait_ge(base_ready, 1)
            wide = load_wide(act)
            with act.If(wide > 0):
                with act.Fori(0, G * NW) as n:
                    onehot_cast(0, n + WIDE, 1)

            def root(v, r, turn):
                act.wait_ge(var_ready, turn)
                act.activation(r[:, :], v[:, :], ACT.Ln).then_inc(log_ready, 1)
                act.wait_ge(log_ready, turn)
                act.activation(r[:, :], r[:, :], ACT.Exp, scale=-0.5).then_inc(root_ready, 1)

            root(var, rstd, 1)
            with act.Fori(0, CHUNKS) as c:
                act.wait_ge(h1_turned, c)
                act.wait_ge(stats_ready, 1)
                for t in range(CT):
                    a = act.activation(h1[:, t, :], X[:, bass.ds(c * CT + t, 1), :].squeeze(1), ACT.Relu,
                                       bias=shift[:, bass.ds(c * CT + t, 1)], scale=rstd[:, bass.ds(c * CT + t, 1)])
                a.then_inc(h1_ready, 1)
                act.wait_ge(h1_turned, c + 1)
                act.wait_ge(update_ready, c)
                act.activation(h1T[:, :, 0:NT], node_tiles(pA, NT), ACT.Copy).then_inc(h1T_ready, 1)
                act.wait_ge(update_ready, c + 1)
                act.wait_ge(x1_ready, c)
                act.activation(softp, node_tiles(pB)[0:NT], ACT.Abs).then_inc(softp_step, 1)
                act.wait_ge(softp_step, c * 2 + 1)
                act.activation(softp, softp, ACT.Exp, scale=-1.0).then_inc(softp_step, 1)
                act.wait_ge(softp_step, c * 2 + 2)
                act.activation(softp, softp, ACT.Ln, bias=1.0).then_inc(softp_ready, 1)
                root(var2, rstd2, c + 2)
                act.wait_ge(ln2_ready, c + 1)
                act.wait_ge(h2_turned, c)
                act.wait_ge(h2_stored, c * 16)
                act.sem_inc(h2_turn, 1)
                for t in range(CT):
                    a = act.activation(h2[:, t, :], X[:, bass.ds(c * CT + t, 1), :].squeeze(1), ACT.Relu,
                                       bias=shift2[:, t:t + 1], scale=rstd2[:, t:t + 1])
                a.then_inc(h2_ready, 1)
                act.wait_ge(qk_ready, c + 1)
                act.wait_ge(stats_ready, 1)
                act.activation(QK[:, bass.ds(c * CN, CN)], two_banks(pD)[:, 0:CN], ACT.Copy,
                               scale=SCALE).then_inc(qk_stored, 1)

            TURNS = [range(0, 4), range(4, 7), range(7, 10), range(10, 13)]

            def copy_rowsT(m, n):
                for q, tiles in enumerate(TURNS):
                    act.wait_ge(rows_turned, m * 4 + q + 1)
                    if q == 0:
                        wait_if(act, scores_ready, n)
                    a, b = tiles[0], tiles[-1] + 1
                    act.activation(rowsT[:, a:b, :],
                                   pA[:, q % 2, 0:(b - a) * P].rearrange("p (j e) -> p j e", e=P),
                                   ACT.Copy).then_inc(rowsT_ready, 1)

            def exps(slot, n, lag):
                act.wait_ge(drop_ready, n + 1)
                wait_if(act, scaled, 2 * (n - lag + 1))
                act.activation(rescale[:, slot], drop[:, :], ACT.Exp).then_inc(rescale_ready, 1)
                act.wait_ge(centred_ready, n + 1)
                act.activation(centred[:, :, :], centred[:, :, :], ACT.Exp).then_inc(exp_ready, 1)

            copy_rowsT(0, 0)
            exps(0, 0, 2)
            copy_rowsT(1, 1)
            exps(1, 1, 2)
            with act.Fori(1, G // 2) as k:
                for i in range(2):
                    g = k * 2 + i
                    copy_rowsT(g, g)
                    exps(i, g, 2)
            with act.If(wide > 0):
                with act.Fori(0, G) as g:
                    copy_rowsT(g + G, g * NW + WIDE)
                    with act.Fori(0, NW) as w:
                        exps(0, g * NW + w + WIDE, 1)

        @block.vector
        def _(dve):
            dve.wait_ge(dst_loaded, 32)
            dve.tensor_copy(dst_f[:, :], dst_i).then_inc(prep, 1)
            dve.wait_ge(prep, 1)
            by_group = dst_f[:, :].rearrange("p (g j) -> p g j", j=J)
            dve.tensor_reduce(low_p[:, :], by_group, AX.X, ALU.min).then_inc(prep, 1)
            dve.tensor_reduce(high_p[:, :], by_group, AX.X, ALU.max).then_inc(prep, 1)

            dve.wait_ge(weight_turned, 1)
            dve.tensor_copy(WnT[:, :], pA[:, 0, 0:P]).then_inc(weight_copied, 1)
            dve.tensor_copy(WeT[:, :], pA[:, 0, P:2 * P]).then_inc(weight_copied, 1)
            dve.tensor_copy(WgT[:, :], pA[0:GF, 0, 2 * P:3 * P]).then_inc(weight_copied, 1)
            dve.tensor_copy(WpT[:, :], pA[:, 0, 3 * P:4 * P]).then_inc(weight_copied, 1)
            dve.wait_ge(weight_turned, 2)
            dve.tensor_copy(Wqk[:, :], pA[:, 1, 0:P]).then_inc(weight_copied, 1)
            dve.tensor_copy(g0_rep[:, :], g0[:, :].to_broadcast([GF, NT])).then_inc(weight_copied, 1)

            dve.wait_ge(bounds_turned, 1)
            dve.tensor_reduce(low[:, :], pD[0:G, 0, 0:P], AX.X, ALU.min).then_inc(prep, 1)
            dve.tensor_reduce(high[:, :], pD[0:G, 0, P:2 * P], AX.X, ALU.max).then_inc(prep, 1)
            dve.wait_ge(prep, 5)
            dve.wait_ge(const_made, 6)
            dve.tensor_scalar(low_diag[:, :], ident[0:G, 0:G], low[:, 0:1], None, ALU.mult).then_inc(prep, 1)
            dve.wait_ge(bounds_turned, 3)
            dve.tensor_copy(base_i[:, :], pD[0:1, 1, 0:G]).then_inc(prep, 1)
            dve.tensor_copy(span_row[:, :], pD[0:1, 1, 0:G]).then_inc(prep, 1)
            dve.wait_ge(prep, 8)
            dve.tensor_tensor(span_row[:, :], pD[0:1, 1, P:P + G], span_row[:, :], ALU.subtract).then_inc(prep, 1)
            dve.wait_ge(prep, 9)
            dve.tensor_reduce(widest[:, :], span_row[:, :], AX.X, ALU.max).then_inc(prep, 1)
            dve.wait_ge(prep, 10)
            dve.tensor_scalar(wide_i[:, :], widest[:, :], float(W), None, ALU.is_ge).then_inc(base_ready, 1)
            dve.wait_ge(repeated_masked, 1)
            dve.tensor_tensor(dst_w[:, :].rearrange("p (g j) -> p g j", j=J), by_group,
                              pD[:, 1, 0:G].unsqueeze(2).to_broadcast([P, G, J]), ALU.subtract).then_inc(prep, 1)
            dve.wait_ge(weight_turned, 3)
            dve.tensor_copy(Wvp[:, :], pB[:, 0, 0:P]).then_inc(weight_copied, 1)
            dve.wait_ge(prep, 11)
            dve.wait_ge(zeroed, 2)

            def make_onehot(slot, cols, n, lag, ready):
                wait_if(dve, sums_ready, n - lag + 1)
                wait_if(dve, onehot16_ready, n - lag + 1)
                dve.tensor_tensor(onehot[:, slot], over_tiles(window_iota[:, :]), over_window(cols),
                                  ALU.is_equal).then_inc(ready, 1)

            def add_sums(slot, base, n):
                dve.wait_ge(sums_ready, n + 1)
                wait_if(dve, sums_added, n)
                a = acc[:, bass.ds(base, W)]
                dve.tensor_tensor(a, a, pA[:, slot, 0:W], ALU.add).then_inc(sums_added, 1)
                dve.wait_ge(counts_ready, n + 1)
                wait_if(dve, counts_added, n)
                a = norm[:, bass.ds(base, W)]
                dve.tensor_tensor(a, a, pB[:, slot, 0:W], ALU.add).then_inc(counts_added, 1)

            def group_cols(t, g):
                return t[:, bass.ds(g * J, J)]

            make_onehot(0, group_cols(dst_w, 0), 0, 2, onehot_ready)
            make_onehot(1, group_cols(dst_w, 1), 1, 2, onehot_ready)
            add_sums(0, load_base(dve, 0), 0)
            with dve.Fori(1, G // 2) as k:
                for i in range(2):
                    g = k * 2 + i
                    make_onehot(i, group_cols(dst_w, g), g, 2, onehot_ready)
                    add_sums(1 - i, load_base(dve, g - 1), g - 1)
            add_sums(1, load_base(dve, G - 1), G - 1)

            wide = load_wide(dve)

            def next_window(step_sem):
                dve.tensor_scalar(rel[:, :], rel[:, :], float(W), None, ALU.subtract).then_inc(step_sem, 1)

            with dve.If(wide > 0):
                dve.tensor_scalar(wide_f, dst_f[:, :], 1.0, None, ALU.add).then_inc(wide_step, 1)
                dve.wait_ge(wide_step, 1)
                dve.scalar_tensor_tensor(out=wide_f, in0=dst_w[:, :], scalar=float(W), in1=wide_f, op0=ALU.is_ge,
                                         op1=ALU.mult).then_inc(wide_step, 1)
                dve.wait_ge(wide_step, 2)
                dve.tensor_scalar(wide_f, wide_f, 1.0, None, ALU.subtract).then_inc(wide_step, 1)
                dve.wait_ge(wide_step, 3)
                with dve.Fori(0, G) as g:
                    dve.wait_ge(onehot_ready, g * NW + WIDE)
                    dve.tensor_copy(rel[:, :], group_cols(wide_f, g)).then_inc(wide_step, 1)
                    with dve.Fori(0, NW) as w:
                        n = g * NW + w + WIDE
                        dve.wait_ge(wide_step, g * (NW + 1) + w + 4)
                        make_onehot(0, rel[:, :], n, 1, onehot_ready)
                        dve.wait_ge(onehot_ready, n + 1)
                        next_window(wide_step)
                        add_sums(0, w * W, n)

            dve.wait_ge(x_loaded, 16)
            with dve.Fori(0, CHUNKS) as c:
                for t in range(CT):
                    dve.bn_stats(ln1[0][:, bass.ds(c * CT + t, 1), :].squeeze(1),
                                 X[:, bass.ds(c * CT + t, 1), :].squeeze(1)).then_inc(ln_step, 1)

            def ln_scale(tiles, turn, before, done):
                st, mean2, diff, var, r, sh = (t[:, :] if len(t.shape) == 2 else t for t in tiles)
                a, b = st[:, :, 1], st[:, :, 4]
                dve.wait_ge(ln_step, before)
                dve.tensor_tensor(mean2, a, b, ALU.add).then_inc(ln_step, 1)
                dve.tensor_tensor(diff, a, b, ALU.subtract).then_inc(ln_step, 1)
                dve.tensor_tensor(var, st[:, :, 2], st[:, :, 5], ALU.add).then_inc(ln_step, 1)
                dve.wait_ge(ln_step, before + 3)
                dve.tensor_tensor(diff, diff, diff, ALU.mult).then_inc(ln_step, 1)
                dve.wait_ge(ln_step, before + 4)
                dve.scalar_tensor_tensor(out=var, in0=diff, scalar=D / 4.0, in1=var,
                                         op0=ALU.mult, op1=ALU.add).then_inc(ln_step, 1)
                dve.wait_ge(ln_step, before + 5)
                dve.tensor_scalar(var, var, 1.0 / D, LN_EPS, ALU.mult, ALU.add).then_inc(var_ready, 1)
                dve.wait_ge(root_ready, turn)
                dve.tensor_tensor(diff, r, r, ALU.mult).then_inc(ln_step, 1)
                dve.wait_ge(ln_step, before + 6)
                dve.tensor_tensor(diff, diff, var, ALU.mult).then_inc(ln_step, 1)
                dve.wait_ge(ln_step, before + 7)
                dve.tensor_scalar(diff, diff, -0.5, 1.5, ALU.mult, ALU.add).then_inc(ln_step, 1)
                dve.wait_ge(ln_step, before + 8)
                dve.tensor_tensor(r, r, diff, ALU.mult).then_inc(ln_step, 1)
                dve.wait_ge(ln_step, before + LN_STEPS)
                dve.scalar_tensor_tensor(out=sh, in0=mean2, scalar=-0.5, in1=r,
                                         op0=ALU.mult, op1=ALU.mult).then_inc(done, 1)

            ln_scale(ln1, 1, TILES, stats_ready)
            dve.wait_ge(counts_added, G)
            dve.tensor_scalar(norm[:, :], norm[:, :], 1.0, None, ALU.max).then_inc(inverse_ready, 1)
            dve.wait_ge(inverse_ready, 1)
            dve.reciprocal(norm[:, :], norm[:, :]).then_inc(inverse_ready, 1)
            dve.wait_ge(inverse_ready, 2)
            dve.wait_ge(sums_added, G)

            dve.wait_ge(stats_ready, 1)
            with dve.Fori(0, CHUNKS) as c:
                dve.wait_ge(update_ready, c)
                dve.tensor_tensor(meanT[:, :, 0:NT],
                                  acc[:, bass.ds(c * CN, CN)].rearrange("p (t n) -> p t n", n=NT),
                                  norm[:, bass.ds(c * CN, CN)].rearrange("p (t n) -> p t n", n=NT),
                                  ALU.mult).then_inc(meanT_ready, 1)
                dve.wait_ge(softp_ready, c + 1)
                dve.scalar_tensor_tensor(out=softp, in0=node_tiles(pB)[0:NT], scalar=0.0, in1=softp,
                                         op0=ALU.max, op1=ALU.add).then_inc(softp_summed, 1)
                dve.wait_ge(softp_summed, c + 1)
                xc = X[:, bass.ds(c * CT, CT), :]
                dve.scalar_tensor_tensor(out=xc, in0=softp, scalar=-LN2, in1=xc,
                                         op0=ALU.add, op1=ALU.add).then_inc(x1_ready, 1)
                dve.wait_ge(stats_ready, 1)
                dve.wait_ge(x1_ready, c + 1)
                for t in range(CT):
                    dve.bn_stats(ln2[0][:, t, :], X[:, bass.ds(c * CT + t, 1), :].squeeze(1)).then_inc(ln_step, 1)
                dve.wait_ge(h2_ready, c)
                ln_scale(ln2, c + 2, c * (CT + LN_STEPS) + TILES + LN_STEPS + CT, ln2_ready)
                dve.wait_ge(h2_turned, c + 1)
                dve.wait_ge(qk_ready, c)
                dve.tensor_copy(h2T_flat.rearrange("p (t n) -> p t n", n=NT), node_tiles(pC, NT)) \
                    .then_inc(h2T_ready, 1)

            dve.wait_ge(cleared, 3)

            def mask_scores(slot, cols, n, lag):
                wait_if(dve, probs_ready, n - lag + 1)
                dve.tensor_tensor(onehot[:, slot], over_tiles(window_iota[:, :]), over_window(cols),
                                  ALU.is_equal).then_inc(hot_ready, 1)
                dve.wait_ge(hot_ready, n + 1)
                wait_if(dve, masked_ready, n)
                dve.tensor_scalar(unmask[:, :, :], onehot[:, slot], 1.0, BIG, ALU.subtract, ALU.mult) \
                    .then_inc(unmask_ready, 1)
                dve.wait_ge(unmask_ready, n + 1)
                dve.wait_ge(scores_ready, n + 1)
                wait_if(dve, centred_ready, n)
                dve.tensor_tensor(masked[:, :, :], scores_ps[slot], unmask[:, :, :], ALU.add) \
                    .then_inc(masked_ready, 1)
                dve.wait_ge(masked_ready, n + 1)
                wait_if(dve, top_turned, n)
                dve.tensor_reduce(tile_top[:, 0:W], masked[:, :, :].rearrange("p j n -> p n j"), AX.X, ALU.max) \
                    .then_inc(tile_top_ready, 1)

            def softmax_step(slot, base, n, lag):
                dve.wait_ge(top_turned, n + 1)
                dve.tensor_reduce(group_top[:, :], turned_ps[0:W, :], AX.X, ALU.max).then_inc(group_top_ready, 1)
                dve.wait_ge(group_top_ready, n + 1)
                wait_if(dve, top_spread, n)
                dve.tensor_scalar(top_diag[:, :], ident[0:W, 0:W], group_top[:, 0:1], None, ALU.mult) \
                    .then_inc(top_diag_ready, 1)
                dve.wait_ge(top_spread, n + 1)
                wait_if(dve, top_stored, n)
                wait_if(dve, centred_ready, n)
                window_top = top[:, bass.ds(base, W)]
                dve.tensor_tensor(new_top[:, :], window_top, spread_ps, ALU.max).then_inc(new_top_ready, 1)
                dve.wait_ge(new_top_ready, n + 1)
                wait_if(dve, rescale_ready, n)
                dve.tensor_tensor(drop[:, :], window_top, new_top[:, :], ALU.subtract).then_inc(drop_ready, 1)
                wait_if(dve, probs_ready, n)
                dve.tensor_tensor(centred[:, :, :], masked[:, :, :], over_tiles(new_top[:, :]), ALU.subtract) \
                    .then_inc(centred_ready, 1)
                dve.wait_ge(drop_ready, n + 1)
                dve.tensor_scalar(window_top, new_top[:, :], 0.0, None, ALU.add).then_inc(top_stored, 1)
                dve.wait_ge(exp_ready, n + 1)
                wait_if(dve, agg_ready, n)
                dve.scalar_tensor_tensor(out=probs[:, :, :], in0=centred[:, :, :], scalar=CLIP,
                                         in1=onehot[:, slot], op0=ALU.max, op1=ALU.mult).then_inc(probs_ready, 1)

            def add_aggregate(slot, base, n):
                dve.wait_ge(agg_ready, n + 1)
                dve.wait_ge(rescale_ready, n + 1)
                wait_if(dve, agg_added, 2 * n)
                a, s = acc[:, bass.ds(base, W)], norm[:, bass.ds(base, W)]
                dve.tensor_tensor(a, a, rescale[:, slot], ALU.mult).then_inc(scaled, 1)
                dve.tensor_tensor(s, s, rescale[:, slot], ALU.mult).then_inc(scaled, 1)
                dve.wait_ge(scaled, n * 2 + 2)
                dve.tensor_tensor(a, a, agg_ps, ALU.add).then_inc(agg_added, 1)
                dve.tensor_tensor(s, s, sum_ps, ALU.add).then_inc(agg_added, 1)

            mask_scores(0, group_cols(dst_w, 0), 0, 2)
            softmax_step(0, load_base(dve, 0), 0, 2)
            mask_scores(1, group_cols(dst_w, 1), 1, 2)
            add_aggregate(0, load_base(dve, 0), 0)
            softmax_step(1, load_base(dve, 1), 1, 2)
            with dve.Fori(1, G // 2) as k:
                for i in range(2):
                    g = k * 2 + i
                    mask_scores(i, group_cols(dst_w, g), g, 2)
                    add_aggregate(1 - i, load_base(dve, g - 1), g - 1)
                    softmax_step(i, load_base(dve, g), g, 2)
            add_aggregate(1, load_base(dve, G - 1), G - 1)
            with dve.If(wide > 0):
                with dve.Fori(0, G) as g:
                    dve.wait_ge(hot_ready, g * NW + WIDE)
                    dve.tensor_copy(rel[:, :], group_cols(wide_f, g)).then_inc(wide2_step, 1)
                    with dve.Fori(0, NW) as w:
                        n = g * NW + w + WIDE
                        dve.wait_ge(wide2_step, g * (NW + 1) + w + 1)
                        mask_scores(0, rel[:, :], n, 1)
                        next_window(wide2_step)
                        softmax_step(0, w * W, n, 1)
                        add_aggregate(0, w * W, n)
                dve.wait_ge(agg_added, 2 * (WIDE + G * NW))

            dve.wait_ge(agg_added, 2 * G)
            dve.tensor_scalar(norm[:, :], norm[:, :], 1e-9, None, ALU.add).then_inc(sum_inverted, 1)
            dve.wait_ge(sum_inverted, 1)
            dve.reciprocal(norm[:, :], norm[:, :]).then_inc(sum_inverted, 1)
            dve.wait_ge(sum_inverted, 2)
            with dve.Fori(0, CHUNKS // 2) as k:
                for i in range(2):
                    c = k * 2 + i
                    dve.wait_ge(out_mm, c)
                    dve.tensor_tensor(aggT[i][:, :, 0:NT],
                                      acc[:, bass.ds(c * CN, CN)].rearrange("p (t n) -> p t n", n=NT),
                                      norm[:, bass.ds(c * CN, CN)].rearrange("p (t n) -> p t n", n=NT),
                                      ALU.mult).then_inc(aggT_ready, 1)
                    dve.wait_ge(out_mm, c + 1)
                    dve.wait_ge(h_in_loaded[i], (k + 1) * 16)
                    dve.wait_ge(out_stored[i], k * 16)
                    dve.tensor_tensor(y[i], node_tiles((pB, pC)[i])[0:NT], h_in[i], ALU.add).then_inc(y_step, 1)
                    dve.wait_ge(y_step, c + 1)
                    dve.scalar_tensor_tensor(out=y[i], in0=y[i], scalar=0.0, in1=X[:, bass.ds(c * CT, CT), :],
                                             op0=ALU.max, op1=ALU.add).then_inc(y_ready, 1)


_INS = ["x", "src", "dst", "edge_attr_128", "L0_gnn_global_feats", "L0_gnn_W", "L1_gnn_Wq", "L1_gnn_Wk",
        "L1_gnn_Wv", "L1_gnn_Wp", "L1_gnn_bp"]


def kernel(**inputs):
    import numpy as _np
    import concourse.bacc as _bacc
    from concourse import mybir as _mybir
    from concourse.bass_utils import run_bass_kernel_spmd as _run

    nc = _bacc.Bacc("TRN2", target_bir_lowering=False, num_devices=1)
    arrays, args = {}, []
    for name in _INS:
        a = _np.ascontiguousarray(inputs[name])
        arrays[f"in_{name}_dram"] = a
        args.append(nc.dram_tensor(f"in_{name}_dram", a.shape, _mybir.dt.from_np(a.dtype), kind="ExternalInput").ap())
    out = nc.dram_tensor("out_dram", inputs["x"].shape, F32, kind="ExternalOutput").ap()
    build(nc, *args, out)
    r = _run(nc, [arrays], core_ids=[0])
    return r.results[0]["out_dram"]
```

```python
from contextlib import ExitStack

import concourse.bass as bass
from concourse import mybir

F32 = mybir.dt.float32
BF16 = mybir.dt.bfloat16
I32 = mybir.dt.int32
ALU = mybir.AluOpType
ACT = mybir.ActivationFunctionType
AX = mybir.AxisListType

P = 128
J = 13
GROUP = P * J
W = 58
WS = 64
NT = 125
CT = 5
POOL_TILES = 11
RING = 4
BIG = 1.0e30
CLIP = 1.9287498479639178e-22
LN_EPS = 1e-5
LN_STEPS = 9
LN2 = 0.6931471805599453


def build(nc, x, src, dst, edge_attr, global_feats, W0, Wq, Wk, Wv, Wp, bp, out):
    N, D = x.shape
    E = src.shape[0]
    GF = global_feats.shape[1]
    assert D == P and N % (NT * CT) == 0
    G = -(-E // GROUP)
    LAST = E - GROUP
    REPEATED = (G - 1) * GROUP - LAST
    assert G % RING == 0 and G % 2 == 0 and 0 <= REPEATED < GROUP and G <= P
    TILES = N // NT
    CHUNKS = TILES // CT
    CN = CT * NT
    NW = -(-N // W)
    FIRST = 512
    NPAD = N + W
    SCALE = float(D) ** -0.5

    x_t = x.rearrange("(t p) d -> p t d", p=NT)
    out_t = out.rearrange("(t p) d -> p t d", p=NT)

    def group_edges(g):
        return edge_attr[bass.ds(g * GROUP, GROUP), :].rearrange("(p j) d -> p j d", j=J)

    def group_sources(g):
        return src[bass.ds(g * GROUP, GROUP)].rearrange("(p j) -> p j", j=J)

    with ExitStack() as ctx:
        def sb(name, shape, dt=F32):
            return ctx.enter_context(nc.sbuf_tensor(name, shape, dt))

        def ps(name, shape, dt=F32):
            return ctx.enter_context(nc.psum_tensor(name, shape, dt))

        def sem(name):
            return ctx.enter_context(nc.semaphore(name))

        h_table = nc.dram_tensor("h_table", [N, D], F32, kind="Internal").ap()
        h_table_t = h_table.rearrange("(t p) d -> p t d", p=NT)

        ident = sb("ident", [P, P])
        ones = sb("ones", [P, P])
        ones16 = sb("ones16", [P, P], BF16)
        window_iota = sb("window_iota", [P, W])
        WnT = sb("WnT", [P, P])
        WeT = sb("WeT", [P, P])
        WgT = sb("WgT", [GF, P])
        WpT = sb("WpT", [P, P])
        Wqk = sb("Wqk", [P, P])
        Wvp = sb("Wvp", [P, P])
        g0 = sb("g0", [GF, 1])
        global_part = sb("global_part", [P, 1])
        bp_rep = sb("bp_rep", [NT, P])

        dst_f = sb("dst_f", [P, G * J])
        dst_w = sb("dst_w", [P, G * J])
        wide_f = dst_f[:, :]
        rel = sb("rel", [P, J])
        low_p = sb("low_p", [P, G])
        high_p = sb("high_p", [P, G])
        low = sb("low", [G, 1])
        high = sb("high", [G, 1])
        low_diag = sb("low_diag", [G, G])
        base_i = sb("base_i", [1, G], I32)
        span_row = sb("span_row", [1, G])
        widest = sb("widest", [1, 1])
        wide_i = sb("wide_i", [1, 1], I32)

        X = sb("X", [NT, TILES, D])
        sums_norms = sb("sums_norms", [P, 2, NPAD])
        acc = sums_norms[:, 0, :]
        norm = sums_norms[:, 1, :]
        top = sb("top", [P, NPAD])
        QK = sb("QK", [P, NPAD])

        dst_i = QK[:, 0:G * J].bitcast(I32)
        W0_sb = QK[:, G * J:G * J + 2 * D + GF]
        Wq_sb, Wk_sb, Wv_sb, Wp_sb = (QK[:, N - (i + 1) * P:N - i * P] for i in range(4))

        rows = sb("rows", [P, RING, J, D])
        srcs = sb("srcs", [P, RING, J], I32)

        work = sb("work", [P, 4 * J * P])
        residue = [work[:, i * J * D:(i + 1) * J * D].rearrange("p (j d) -> p j d", d=D) for i in range(2)]
        lowest = [work[:, (4 + i) * J * D // 2:(5 + i) * J * D // 2].bitcast(BF16)
                  .rearrange("p (j d) -> p j d", d=D) for i in range(2)]
        onehot16 = [work[:, 3 * J * D + i * J * W // 2:3 * J * D + (i + 1) * J * W // 2].bitcast(BF16)
                    .rearrange("p (j n) -> p j n", n=W) for i in range(RING)]

        def upper(t):
            return t.bitcast(BF16)[:, :, 1:2 * D:2]

        rowsT = work[:, 0:J * P].rearrange("p (j e) -> p j e", e=P)
        unmask, masked, centred, probs = (
            work[:, J * P + i * J * W:J * P + (i + 1) * J * W].rearrange("p (j n) -> p j n", n=W)
            for i in range(4))
        onehot = sb("onehot", [P, 2, J, W])
        tile_top = sb("tile_top", [P, P])
        group_top = sb("group_top", [W, 1])
        prob_sum = sb("prob_sum", [P, W])
        new_top = sb("new_top", [P, W])
        drop = sb("drop", [P, W])
        inverse = sb("inverse", [NT, 2, CT])
        rescale = sb("rescale", [P, 2, W])

        def ln_tiles(name, n):
            return [sb(f"{name}_stats", [NT, n, 6])] + \
                [sb(f"{name}_{what}", [NT, n]) for what in ("mean2", "diff", "var", "rstd", "shift")]

        ln1 = ln_tiles("ln1", TILES)
        ln2 = ln_tiles("ln2", CT)
        var, rstd, shift = ln1[3:]
        var2, rstd2, shift2 = ln2[3:]

        def chunk_buffer(slot, half, parts=P):
            return rows[0:parts, slot].rearrange("p j d -> p (j d)")[:, half * 6 * D:half * 6 * D + CT * D]\
                .rearrange("p (t d) -> p t d", d=D)

        def flat(chunk):
            return chunk.rearrange("p t d -> p (t d)")[:, 0:CN]

        def by_tile(flat_chunk):
            return flat_chunk.rearrange("p (t n) -> p t n", n=NT)

        h1 = chunk_buffer(0, 0, NT)
        h1T = flat(chunk_buffer(0, 1))
        softp = flat(chunk_buffer(1, 0))
        positive = flat(chunk_buffer(1, 1))
        h2 = chunk_buffer(2, 0, NT)
        h2T = flat(chunk_buffer(2, 1))
        agg_sumT = [rows[:, i].rearrange("p j d -> p (j d)")[:, 0:2 * CN].rearrange("p (s n) -> p s n", n=CN)
                    for i in range(2)]
        h_in = [chunk_buffer(2, 0, NT), chunk_buffer(2, 1, NT)]
        y = [chunk_buffer(3, 0, NT), chunk_buffer(3, 1, NT)]

        pA = ps("pA", [P, 2, 512])
        pB = ps("pB", [P, 2, 512])
        pC = ps("pC", [P, 2, 512])
        pD = ps("pD", [P, 2, 512])

        def two_banks(t):
            return t[:, :, :].rearrange("p b n -> p (b n)")

        def node_tiles(t, width=P):
            return two_banks(t)[:, 0:CT * P].rearrange("p (t d) -> p t d", d=P)[:, :, 0:width]

        scores_ps = [two_banks(t)[:, 0:J * WS].rearrange("p (j n) -> p j n", n=WS)[:, :, 0:W] for t in (pB, pC)]
        turned_ps = pD[:, 0, 0:P]
        spread_ps = pD[:, 0, P:P + W]
        agg_ps = pD[:, 1, 0:W]

        dst_loaded = sem("dst_loaded")
        x_loaded = sem("x_loaded")
        weights_loaded = sem("weights_loaded")
        edges_loaded = [sem(f"edges_loaded{i}") for i in range(RING)]
        const_made = sem("const_made")
        zeroed = sem("zeroed")
        weight_turned = sem("weight_turned")
        weight_copied = sem("weight_copied")
        prep = sem("prep")
        bounds_turned = sem("bounds_turned")
        repeated_masked = sem("repeated_masked")
        base_ready = sem("base_ready")

        onehot_ready = sem("onehot_ready")
        residue_ready = sem("residue_ready")
        lowest_ready = sem("lowest_ready")
        lowest_rest_ready = sem("lowest_rest_ready")
        sums_ready = sem("sums_ready")
        sums_added = sem("sums_added")
        wide_step = sem("wide_step")

        ln_step = sem("ln_step")
        stats_ready = sem("stats_ready")
        var_ready = sem("var_ready")
        log_ready = sem("log_ready")
        root_ready = sem("root_ready")
        counts_bounded = sem("counts_bounded")
        invert_turn = sem("invert_turn")
        inverse_ready = sem("inverse_ready")
        h1_ready = sem("h1_ready")
        h1_turned = sem("h1_turned")
        h1T_ready = sem("h1T_ready")
        mean_turn = sem("mean_turn")
        mean_ready = sem("mean_ready")
        update_ready = sem("update_ready")
        softp_step = sem("softp_step")
        softp_ready = sem("softp_ready")
        positive_ready = sem("positive_ready")
        softp_summed = sem("softp_summed")
        softp_turned = sem("softp_turned")
        x1_ready = sem("x1_ready")
        ln2_ready = sem("ln2_ready")
        h2_turn = sem("h2_turn")
        h2_ready = sem("h2_ready")
        h2_stored = sem("h2_stored")
        h2_turned = sem("h2_turned")
        h2T_ready = sem("h2T_ready")
        qk_ready = sem("qk_ready")
        qk_stored = sem("qk_stored")

        cleared = sem("cleared")
        qk_padded = sem("qk_padded")
        srcs_loaded = [sem(f"srcs_loaded{i}") for i in range(RING)]
        gather_turn = sem("gather_turn")
        gathered = [sem(f"gathered{i}") for i in range(RING)]
        rows_turned = sem("rows_turned")
        rowsT_ready = sem("rowsT_ready")
        scores_ready = sem("scores_ready")
        hot_ready = sem("hot_ready")
        unmask_ready = sem("unmask_ready")
        masked_ready = sem("masked_ready")
        tile_top_ready = sem("tile_top_ready")
        top_turned = sem("top_turned")
        group_top_ready = sem("group_top_ready")
        top_spread = sem("top_spread")
        new_top_ready = sem("new_top_ready")
        drop_ready = sem("drop_ready")
        rescale_ready = sem("rescale_ready")
        top_stored = sem("top_stored")
        centred_ready = sem("centred_ready")
        exp_ready = sem("exp_ready")
        probs_ready = sem("probs_ready")
        prob_sum_ready = sem("prob_sum_ready")
        agg_ready = sem("agg_ready")
        scaled = sem("scaled")
        agg_added = sem("agg_added")
        wide2_step = sem("wide2_step")

        norm_added = sem("norm_added")
        all_added = sem("all_added")
        sum_mm = sem("sum_mm")
        sum_bounded = sem("sum_bounded")
        sum_inverted = sem("sum_inverted")
        aggT_ready = sem("aggT_ready")
        bias_added = sem("bias_added")
        h_in_loaded = [sem(f"h_in_loaded{i}") for i in range(2)]
        out_mm = sem("out_mm")
        y_step = sem("y_step")
        y_ready = sem("y_ready")
        out_stored = [sem(f"out_stored{i}") for i in range(2)]

        GATHER = 16 * J
        WIDE = G

        def wait_if(eng, s, value):
            if not isinstance(value, int) or value > 0:
                eng.wait_ge(s, value)

        def over_tiles(row, n=W):
            return row.unsqueeze(1).to_broadcast([P, J, n])

        def over_window(cols):
            return cols.unsqueeze(2).to_broadcast([P, J, W])

        def load_base(eng, g):
            return eng.value_load(base_i[0:1, bass.ds(g, 1)], min_val=0, max_val=N - 1)

        def load_wide(eng):
            return eng.value_load(wide_i[0:1, 0:1], min_val=0, max_val=1)

        block = ctx.enter_context(nc.Block())

        @block.sync
        def _(sp):
            sp.dma_start(dst_i[:, 0:(G - 1) * J].rearrange("p (g j) -> p g j", j=J),
                         dst[0:(G - 1) * GROUP].rearrange("(g p j) -> p g j", p=P, j=J)).then_inc(dst_loaded, 16)
            sp.dma_start(dst_i[:, (G - 1) * J:G * J],
                         dst[LAST:E].rearrange("(p j) -> p j", j=J)).then_inc(dst_loaded, 16)
            for tile, source in ((W0_sb, W0), (Wq_sb, Wq), (Wk_sb, Wk), (Wv_sb, Wv), (Wp_sb, Wp)):
                sp.dma_start(tile[:, :], source).then_inc(weights_loaded, 16)
            sp.dma_start(bp_rep[:, :], bp.unsqueeze(0).to_broadcast([NT, P])).then_inc(weights_loaded, 16)
            sp.dma_start(g0[:, :], global_feats[0:1, :].rearrange("a f -> f a")).then_inc(weights_loaded, 16)
            sp.dma_start(X[:, :, :], x_t).then_inc(x_loaded, 16)

            def load_edges(source, slot, free):
                wait_if(sp, sums_ready, free)
                sp.dma_start(rows[:, slot], source).then_inc(edges_loaded[slot], 16)

            for g in range(RING):
                load_edges(group_edges(g), g, 0)
            with sp.Fori(1, G // RING - 1) as k:
                for i in range(RING):
                    load_edges(group_edges(k * RING + i), i, k * RING + (i - RING + 1))
            for g in range(G - RING, G - 1):
                load_edges(group_edges(g), g % RING, g - RING + 1)
            last_edges = edge_attr[LAST:E, :].rearrange("(p j) d -> p j d", j=J)
            load_edges(last_edges, (G - 1) % RING, G - RING)

            sp.wait_ge(base_ready, 1)
            wide = load_wide(sp)
            with sp.If(wide > 0):
                with sp.Fori(0, G - 1) as g:
                    load_edges(group_edges(g), 0, WIDE + g * NW)
                load_edges(last_edges, 0, WIDE + (G - 1) * NW)

            with sp.Fori(0, CHUNKS) as c:
                sp.wait_ge(h2_ready, c + 1)
                sp.dma_start(h_table_t[:, bass.ds(c * CT, CT), :], h2).then_inc(h2_stored, 16)

            def load_sources(source, slot, engine_done):
                for s, value in engine_done:
                    wait_if(sp, s, value)
                sp.dma_start(srcs[:, slot], source).then_inc(srcs_loaded[slot], 16)

            for g in range(RING):
                load_sources(group_sources(g), g, [])
            with sp.Fori(1, G // RING - 1) as k:
                for i in range(RING):
                    load_sources(group_sources(k * RING + i), i, [(gathered[i], k * GATHER)])
            for g in range(G - RING, G - 1):
                load_sources(group_sources(g), g % RING, [(gathered[g % RING], g // RING * GATHER)])
            last_sources = src[LAST:E].rearrange("(p j) -> p j", j=J)
            load_sources(last_sources, (G - 1) % RING, [(gathered[(G - 1) % RING], (G // RING - 1) * GATHER)])
            with sp.If(wide > 0):
                with sp.Fori(0, G - 1) as g:
                    load_sources(group_sources(g), 0, [(gathered[0], (g + G // RING) * GATHER)])
                load_sources(last_sources, 0, [(gathered[0], (G - 1 + G // RING) * GATHER)])

            def load_h(c, slot):
                sp.dma_start(h_in[slot], h_table_t[:, bass.ds(c * CT, CT), :]).then_inc(h_in_loaded[slot], 16)

            def store_y(c, slot):
                sp.wait_ge(y_ready, c + 1)
                sp.dma_start(out_t[:, bass.ds(c * CT, CT), :], y[slot]).then_inc(out_stored[slot], 16)

            sp.wait_ge(all_added, 1)
            load_h(0, 0)
            load_h(1, 1)
            with sp.Fori(0, CHUNKS // 2 - 1) as k:
                for i in range(2):
                    store_y(k * 2 + i, i)
                    load_h(k * 2 + i + 2, i)
            for i in range(2):
                store_y(CHUNKS - 2 + i, i)
            for i in range(2):
                sp.wait_ge(out_stored[i], 16 * (CHUNKS // 2))

        @block.gpsimd
        def _(pool):
            pool.memset(ident[:, :], 0.0).then_inc(const_made, 1)
            pool.memset(ones[:, :], 1.0).then_inc(const_made, 1)
            pool.memset(ones16[:, :], 1.0).then_inc(const_made, 1)
            pool.memset(tile_top[:, :], 0.0).then_inc(const_made, 1)
            pool.iota(window_iota[:, :], pattern=[[1, W]], base=0, channel_multiplier=0,
                      allow_small_or_imprecise_dtypes=True).then_inc(const_made, 1)
            pool.wait_ge(const_made, 5)
            pool.affine_select(out=ident[:, :], in_=ident[:, :], compare_op=ALU.not_equal, fill=1.0, base=0,
                               pattern=[[-1, P]], channel_multiplier=1).then_inc(const_made, 1)
            pool.memset(sums_norms[:, :, :], 0.0).then_inc(zeroed, 1)
            pool.wait_ge(prep, 3)
            pool.affine_select(out=dst_f[:, (G - 1) * J:G * J], in_=dst_f[:, (G - 1) * J:G * J],
                               compare_op=ALU.is_ge, fill=-1.0, base=-REPEATED, pattern=[[1, J]],
                               channel_multiplier=J).then_inc(repeated_masked, 1)
            pool.memset(top[:, :], -BIG).then_inc(cleared, 1)
            pool.memset(QK[:, N:NPAD], 0.0).then_inc(qk_padded, 1)

            def split_lowest(slot, m, used):
                pool.wait_ge(residue_ready, m + 1)
                wait_if(pool, sums_ready, used)
                pool.tensor_tensor(lowest[slot][:, 0:POOL_TILES], residue[slot][:, 0:POOL_TILES],
                                   upper(residue[slot])[:, 0:POOL_TILES], ALU.subtract) \
                    .then_inc(lowest_ready, 1)

            split_lowest(0, 0, 0)
            split_lowest(1, 1, 0)
            with pool.Fori(1, G // 2) as k:
                for i in range(2):
                    split_lowest(i, k * 2 + i, k * 2 + i - 1)
            pool.wait_ge(base_ready, 1)
            wide = load_wide(pool)
            with pool.If(wide > 0):
                with pool.Fori(0, G) as g:
                    split_lowest(0, g + G, g * NW + WIDE)

            with pool.Fori(0, CHUNKS) as c:
                pool.wait_ge(inverse_ready, c + 1)
                pool.sem_inc(mean_turn, 1)
                a = acc[:, bass.ds(c * CN, CN)]
                pool.tensor_tensor(a, a, norm[:, bass.ds(c * CN, CN)], ALU.mult).then_inc(mean_ready, 1)

            pool.wait_ge(update_ready, CHUNKS)
            pool.memset(sums_norms[:, :, :], 0.0).then_inc(cleared, 1)

            last_row = pool.to_reg(N - 1)

            def gather(slot, loads, free):
                pool.wait_ge(srcs_loaded[slot], loads)
                wait_if(pool, agg_ready, free)
                pool.sem_inc(gather_turn, 1)
                for j in range(J):
                    pool.indirect_dma_start(
                        out=rows[:, slot, j, :], out_offset=None, in_=h_table,
                        in_offset=bass.IndirectOffsetOnAxis(ap=srcs[:, slot, j:j + 1], axis=0),
                        bounds_check=last_row).then_inc(gathered[slot], 16)

            pool.wait_ge(h2_stored, 16 * CHUNKS)
            pool.wait_ge(qk_ready, CHUNKS)
            pool.wait_ge(x1_ready, CHUNKS)
            for g in range(RING):
                gather(g, 16, 0)
            with pool.Fori(1, G // RING) as k:
                for i in range(RING):
                    gather(i, (k + 1) * 16, k * RING + (i - RING + 1))
            with pool.If(wide > 0):
                with pool.Fori(0, G) as g:
                    gather(0, (g + G // RING + 1) * 16, WIDE + g * NW)

            def add_bias(slot, c, loads):
                pool.wait_ge(h_in_loaded[slot], loads)
                pool.tensor_tensor(h_in[slot], h_in[slot], bp_rep[:, :].unsqueeze(1).to_broadcast([NT, CT, P]),
                                   ALU.add).then_inc(bias_added, 1)

            for i in range(2):
                add_bias(i, i, 16)
            with pool.Fori(1, CHUNKS // 2) as k:
                for i in range(2):
                    add_bias(i, k * 2 + i, (k + 1) * 16)

        @block.tensor
        def _(pe):
            pe.wait_ge(const_made, 6)
            pe.wait_ge(weights_loaded, 16 * 7)
            pe.transpose(pA[:, 0, 0:P], W0_sb[:, 0:D], ident[:, :])
            pe.transpose(pA[:, 0, P:2 * P], W0_sb[:, D:2 * D], ident[:, :])
            pe.transpose(pA[0:GF, 0, 2 * P:3 * P], W0_sb[:, 2 * D:2 * D + GF], ident[:, :])
            pe.transpose(pA[:, 0, 3 * P:4 * P], Wp_sb[:, :], ident[:, :]).then_inc(weight_turned, 1)
            pe.matmul(pA[:, 1, 0:P], Wq_sb[:, :], Wk_sb[:, :], start=True, stop=True).then_inc(weight_turned, 1)
            pe.wait_ge(weight_copied, 4)
            pe.matmul(pB[:, 0, 0:P], Wv_sb[:, :], WpT[:, :], start=True, stop=True)
            pe.matmul(pB[:, 0, P:P + 1], WgT[:, :], g0[:, :], start=True, stop=True).then_inc(weight_turned, 1)

            pe.wait_ge(prep, 3)
            pe.transpose(pD[0:G, 0, 0:P], low_p[:, :], ident[:, :])
            pe.transpose(pD[0:G, 0, P:2 * P], high_p[:, :], ident[:, :]).then_inc(bounds_turned, 1)
            pe.wait_ge(prep, 6)
            pe.matmul(pD[:, 1, 0:G], ones[0:G, :], low_diag[:, :], start=True, stop=True).then_inc(bounds_turned, 1)
            pe.transpose(pD[0:1, 1, P:P + G], high[:, :], ident[0:G, 0:G]).then_inc(bounds_turned, 1)

            def sums(slot, edge_slot, hot, loads, n, m, lag):
                pe.wait_ge(edges_loaded[edge_slot], loads)
                pe.wait_ge(onehot_ready, n + 1)
                wait_if(pe, sums_added, n - lag + 1)
                for j in range(J):
                    pe.matmul(pA[:, slot, W:2 * W], ones16[:, :], hot[:, j, :], start=(j == 0), stop=(j == J - 1))
                for j in range(J):
                    pe.matmul(pA[:, slot, 0:W], upper(rows[:, edge_slot])[:, j, :], hot[:, j, :],
                              start=(j == 0), stop=False)
                pe.wait_ge(residue_ready, m + 1)
                for j in range(J):
                    pe.matmul(pA[:, slot, 0:W], upper(residue[slot])[:, j, :], hot[:, j, :], start=False, stop=False)
                pe.wait_ge(lowest_ready, m + 1)
                pe.wait_ge(lowest_rest_ready, m + 1)
                for j in range(J):
                    mm = pe.matmul(pA[:, slot, 0:W], lowest[slot][:, j, :], hot[:, j, :],
                                   start=False, stop=(j == J - 1))
                mm.then_inc(sums_ready, 1)

            pe.wait_ge(weight_copied, 7)
            for g in range(RING):
                sums(g % 2, g, onehot16[g], 16, g, g, 2)
            with pe.Fori(1, G // RING) as k:
                for i in range(RING):
                    sums(i % 2, i, onehot16[i], (k + 1) * 16, k * RING + i, k * RING + i, 2)
            pe.wait_ge(base_ready, 1)
            wide = load_wide(pe)
            with pe.If(wide > 0):
                with pe.Fori(0, G) as g:
                    with pe.Fori(0, NW) as w:
                        sums(0, 0, onehot16[0], (g + G // RING + 1) * 16, g * NW + w + WIDE, g + G, 1)

            def turn_h1(c):
                pe.wait_ge(h1_ready, c + 1)
                wait_if(pe, x1_ready, c - 1)
                for t in range(CT):
                    mm = pe.transpose(node_tiles(pA, NT)[:, t, :], h1[:, t, :], ident[0:NT, 0:NT])
                mm.then_inc(h1_turned, 1)

            def project(c):
                pe.wait_ge(h1T_ready, c + 1)
                pe.wait_ge(mean_ready, c + 1)
                wait_if(pe, positive_ready, c)
                for bank, first, n in ((0, 0, FIRST), (1, FIRST, CN - FIRST)):
                    pe.matmul(pB[:, bank, 0:n], WnT[:, :], h1T[:, first:first + n], start=True, stop=False)
                    mm = pe.matmul(pB[:, bank, 0:n], WeT[:, :], acc[:, bass.ds(c * CN + first, n)],
                                   start=False, stop=True)
                mm.then_inc(update_ready, 1)

            def turn_update(c, copied):
                pe.wait_ge(softp_summed, c + 1)
                pe.wait_ge(h1T_ready, copied)
                for t in range(CT):
                    mm = pe.transpose(node_tiles(pA)[0:NT, t, :], by_tile(softp)[:, t, :], ident[:, :])
                mm.then_inc(softp_turned, 1)

            def query(c):
                pe.wait_ge(h2_ready, c + 1)
                wait_if(pe, h2T_ready, c)
                for t in range(CT):
                    mm = pe.transpose(node_tiles(pC, NT)[:, t, :], h2[:, t, :], ident[0:NT, 0:NT])
                mm.then_inc(h2_turned, 1)
                pe.wait_ge(h2T_ready, c + 1)
                wait_if(pe, qk_stored, c)
                pe.matmul(pD[:, 0, 0:FIRST], Wqk[:, :], h2T[:, 0:FIRST], start=True, stop=True)
                pe.matmul(pD[:, 1, 0:CN - FIRST], Wqk[:, :], h2T[:, FIRST:CN],
                          start=True, stop=True).then_inc(qk_ready, 1)

            def update_chunk(c, first, last):
                project(c)
                if not last:
                    turn_h1(c + 1)
                if not first:
                    query(c - 1)
                turn_update(c, c + 1 if last else c + 2)

            pe.wait_ge(sums_added, G)
            turn_h1(0)
            update_chunk(0, True, False)
            with pe.Fori(1, CHUNKS - 1) as c:
                update_chunk(c, False, False)
            update_chunk(CHUNKS - 1, False, True)
            query(CHUNKS - 1)

            pe.wait_ge(qk_stored, CHUNKS)
            pe.wait_ge(qk_padded, 1)
            TURNS = [range(0, 4), range(4, 7), range(7, 10), range(10, 13)]

            def turn_rows(rows_slot, gathers, m, turns):
                if turns[0] == 0:
                    pe.wait_ge(gathered[rows_slot], gathers)
                for q in turns:
                    wait_if(pe, rowsT_ready, m * 4 + q - 1)
                    for a, j in enumerate(TURNS[q]):
                        mm = pe.transpose(pA[:, q % 2, a * P:(a + 1) * P], rows[:, rows_slot, j, :], ident[:, :])
                    mm.then_inc(rows_turned, 1)

            def scores(slot, base, n, m, lag):
                pe.wait_ge(rowsT_ready, m * 4 + 4)
                wait_if(pe, masked_ready, n - lag + 1)
                for j in range(J):
                    mm = pe.matmul(scores_ps[slot][:, j, :], rowsT[:, j, :], QK[:, bass.ds(base, W)],
                                   start=True, stop=True)
                mm.then_inc(scores_ready, 1)

            def turn_top(n):
                pe.wait_ge(tile_top_ready, n + 1)
                wait_if(pe, new_top_ready, n)
                pe.transpose(turned_ps, tile_top[:, :], ident[:, :]).then_inc(top_turned, 1)

            def spread_top(n):
                pe.wait_ge(const_made, 6)
                pe.wait_ge(group_top_ready, n + 1)
                pe.transpose(spread_ps, group_top[:, :].to_broadcast([W, P]), ident[0:W, 0:W]) \
                    .then_inc(top_spread, 1)

            def aggregate(rows_slot, n, tiles):
                if tiles[0] == 0:
                    pe.wait_ge(probs_ready, n + 1)
                    wait_if(pe, agg_added, n)
                for j in tiles:
                    mm = pe.matmul(agg_ps, rows[:, rows_slot, j, :], probs[:, j, :],
                                   start=(j == 0), stop=(j == J - 1))
                if tiles[-1] == J - 1:
                    mm.then_inc(agg_ready, 1)

            ALL, EARLY, LATE = range(J), range(0, 6), range(6, J)

            def edge_step(i, g, next_gathers, first=False, last=False):
                scores(i % 2, load_base(pe, g), g, g, 2)
                if not last:
                    turn_rows((i + 1) % RING, next_gathers, g + 1, (0, 1))
                if not first:
                    aggregate((i - 1) % RING, g - 1, EARLY)
                if not last:
                    turn_rows((i + 1) % RING, next_gathers, g + 1, (2, 3))
                turn_top(g)
                if not first:
                    aggregate((i - 1) % RING, g - 1, LATE)
                spread_top(g)

            turn_rows(0, GATHER, 0, (0, 1, 2, 3))
            for g in range(RING):
                edge_step(g, g, (2 if g == RING - 1 else 1) * GATHER, first=(g == 0))
            with pe.Fori(1, G // RING - 1) as k:
                for i in range(RING):
                    edge_step(i, k * RING + i, (k + (2 if i == RING - 1 else 1)) * GATHER)
            for i in range(RING):
                edge_step(i, G - RING + i, G // RING * GATHER, last=(i == RING - 1))
            aggregate((G - 1) % RING, G - 1, ALL)
            with pe.If(wide > 0):
                with pe.Fori(0, G) as g:
                    turn_rows(0, (g + G // RING + 1) * GATHER, g + G, (0, 1, 2, 3))
                    with pe.Fori(0, NW) as w:
                        n = g * NW + w + WIDE
                        scores(0, w * W, n, g + G, 1)
                        turn_top(n)
                        spread_top(n)
                        aggregate(0, n, ALL)

            def project_aggregate(i, c):
                pe.wait_ge(aggT_ready, c + 1)
                wait_if(pe, y_step, (c - 1) * CT)
                for t in range(CT):
                    mm = pe.matmul(pD[0:NT, i, t:t + 1], by_tile(agg_sumT[i][:, 1, :])[:, t, :], ones[:, 0:1],
                                   start=True, stop=True)
                mm.then_inc(sum_mm, 1)
                for t in range(CT):
                    mm = pe.matmul(node_tiles((pB, pC)[i])[0:NT, t, :], by_tile(agg_sumT[i][:, 0, :])[:, t, :],
                                   Wvp[:, :], start=True, stop=True)
                mm.then_inc(out_mm, 1)

            for i in range(2):
                project_aggregate(i, i)
            with pe.Fori(1, CHUNKS // 2) as k:
                for i in range(2):
                    project_aggregate(i, k * 2 + i)

        @block.scalar
        def _(act):
            act.wait_ge(base_ready, 1)
            wide = load_wide(act)

            def root(v, r, turn):
                act.wait_ge(var_ready, turn)
                act.activation(r[:, :], v[:, :], ACT.Ln).then_inc(log_ready, 1)
                act.wait_ge(log_ready, turn)
                act.activation(r[:, :], r[:, :], ACT.Exp, scale=-0.5).then_inc(root_ready, 1)

            def make_h1(c):
                wait_if(act, h1_turned, c)
                act.wait_ge(stats_ready, 1)
                for t in range(CT):
                    a = act.activation(h1[:, t, :], X[:, bass.ds(c * CT + t, 1), :].squeeze(1), ACT.Relu,
                                       bias=shift[:, bass.ds(c * CT + t, 1)], scale=rstd[:, bass.ds(c * CT + t, 1)])
                a.then_inc(h1_ready, 1)

            def copy_h1T(c):
                act.wait_ge(h1_turned, c + 1)
                wait_if(act, update_ready, c)
                act.activation(by_tile(h1T), node_tiles(pA, NT), ACT.Copy).then_inc(h1T_ready, 1)

            def log_part(c):
                act.wait_ge(update_ready, c + 1)
                wait_if(act, softp_turned, c)
                act.activation(softp, two_banks(pB)[:, 0:CN], ACT.Abs, bias=global_part[:, 0:1]) \
                    .then_inc(softp_step, 1)
                act.wait_ge(softp_step, c * 2 + 1)
                act.activation(softp, softp, ACT.Exp, scale=-1.0).then_inc(softp_step, 1)
                act.wait_ge(softp_step, c * 2 + 2)
                act.activation(softp, softp, ACT.Ln, bias=1.0).then_inc(softp_ready, 1)

            def store_query(c):
                act.wait_ge(qk_ready, c + 1)
                act.wait_ge(stats_ready, 1)
                act.activation(QK[:, bass.ds(c * CN, CN)], two_banks(pD)[:, 0:CN], ACT.Copy,
                               scale=SCALE).then_inc(qk_stored, 1)

            def make_h2(c):
                root(var2, rstd2, c + 2)
                act.wait_ge(ln2_ready, c + 1)
                wait_if(act, h2_turned, c)
                wait_if(act, h2_stored, c * 16)
                act.sem_inc(h2_turn, 1)
                for t in range(CT):
                    a = act.activation(h2[:, t, :], X[:, bass.ds(c * CT + t, 1), :].squeeze(1), ACT.Relu,
                                       bias=shift2[:, t:t + 1], scale=rstd2[:, t:t + 1])
                a.then_inc(h2_ready, 1)

            def update_chunk(c, first=False, after=2):
                log_part(c)
                if after >= 1:
                    copy_h1T(c + 1)
                if after >= 2:
                    make_h1(c + 2)
                if not first:
                    store_query(c - 1)
                make_h2(c)

            root(var, rstd, 1)
            make_h1(0)
            copy_h1T(0)
            make_h1(1)
            update_chunk(0, first=True)
            with act.Fori(1, CHUNKS - 2) as c:
                update_chunk(c)
            update_chunk(CHUNKS - 2, after=1)
            update_chunk(CHUNKS - 1, after=0)
            store_query(CHUNKS - 1)

            TURNS = [range(0, 4), range(4, 7), range(7, 10), range(10, 13)]

            def copy_rowsT(m, n):
                for q, tiles in enumerate(TURNS):
                    act.wait_ge(rows_turned, m * 4 + q + 1)
                    if q == 0:
                        wait_if(act, scores_ready, n)
                    a, b = tiles[0], tiles[-1] + 1
                    act.activation(rowsT[:, a:b, :],
                                   pA[:, q % 2, 0:(b - a) * P].rearrange("p (j e) -> p j e", e=P),
                                   ACT.Copy).then_inc(rowsT_ready, 1)

            def exps(slot, n, lag):
                act.wait_ge(drop_ready, n + 1)
                wait_if(act, scaled, n - lag + 1)
                act.activation(rescale[:, slot], drop[:, :], ACT.Exp).then_inc(rescale_ready, 1)
                act.wait_ge(centred_ready, n + 1)
                act.activation(centred, centred, ACT.Exp).then_inc(exp_ready, 1)

            copy_rowsT(0, 0)
            for g in range(2):
                copy_rowsT(g + 1, g + 1)
                exps(g, g, 2)
            with act.Fori(1, G // 2 - 1) as k:
                for i in range(2):
                    g = k * 2 + i
                    copy_rowsT(g + 1, g + 1)
                    exps(i, g, 2)
            copy_rowsT(G - 1, G - 1)
            exps(0, G - 2, 2)
            exps(1, G - 1, 2)
            with act.If(wide > 0):
                with act.Fori(0, G) as g:
                    copy_rowsT(g + G, g * NW + WIDE)
                    with act.Fori(0, NW) as w:
                        exps(0, g * NW + w + WIDE, 1)

            def copy_sums(i, c):
                wait_if(act, out_mm, c - 1)
                act.wait_ge(all_added, 1)
                act.activation(agg_sumT[i], sums_norms[:, :, bass.ds(c * CN, CN)], ACT.Copy).then_inc(aggT_ready, 1)

            for i in range(2):
                copy_sums(i, i)
            with act.Fori(1, CHUNKS // 2) as k:
                for i in range(2):
                    copy_sums(i, k * 2 + i)

        @block.vector
        def _(dve):
            dve.wait_ge(dst_loaded, 32)
            dve.tensor_copy(dst_f[:, :], dst_i).then_inc(prep, 1)
            dve.wait_ge(prep, 1)
            by_group = dst_f[:, :].rearrange("p (g j) -> p g j", j=J)
            dve.tensor_reduce(low_p[:, :], by_group, AX.X, ALU.min).then_inc(prep, 1)
            dve.tensor_reduce(high_p[:, :], by_group, AX.X, ALU.max).then_inc(prep, 1)

            dve.wait_ge(weight_turned, 1)
            dve.tensor_copy(WnT[:, :], pA[:, 0, 0:P]).then_inc(weight_copied, 1)
            dve.tensor_copy(WeT[:, :], pA[:, 0, P:2 * P]).then_inc(weight_copied, 1)
            dve.tensor_copy(WgT[:, :], pA[0:GF, 0, 2 * P:3 * P]).then_inc(weight_copied, 1)
            dve.tensor_copy(WpT[:, :], pA[:, 0, 3 * P:4 * P]).then_inc(weight_copied, 1)
            dve.wait_ge(weight_turned, 2)
            dve.tensor_copy(Wqk[:, :], pA[:, 1, 0:P]).then_inc(weight_copied, 1)

            dve.wait_ge(bounds_turned, 1)
            dve.tensor_reduce(low[:, :], pD[0:G, 0, 0:P], AX.X, ALU.min).then_inc(prep, 1)
            dve.tensor_reduce(high[:, :], pD[0:G, 0, P:2 * P], AX.X, ALU.max).then_inc(prep, 1)
            dve.wait_ge(prep, 5)
            dve.wait_ge(const_made, 6)
            dve.tensor_scalar(low_diag[:, :], ident[0:G, 0:G], low[:, 0:1], None, ALU.mult).then_inc(prep, 1)
            dve.wait_ge(bounds_turned, 3)
            dve.tensor_copy(base_i[:, :], pD[0:1, 1, 0:G]).then_inc(prep, 1)
            dve.tensor_copy(span_row[:, :], pD[0:1, 1, 0:G]).then_inc(prep, 1)
            dve.wait_ge(prep, 8)
            dve.tensor_tensor(span_row[:, :], pD[0:1, 1, P:P + G], span_row[:, :], ALU.subtract).then_inc(prep, 1)
            dve.wait_ge(prep, 9)
            dve.tensor_reduce(widest[:, :], span_row[:, :], AX.X, ALU.max).then_inc(prep, 1)
            dve.wait_ge(prep, 10)
            dve.tensor_scalar(wide_i[:, :], widest[:, :], float(W), None, ALU.is_ge).then_inc(base_ready, 1)
            dve.wait_ge(repeated_masked, 1)
            dve.tensor_tensor(dst_w[:, :].rearrange("p (g j) -> p g j", j=J), by_group,
                              pD[:, 1, 0:G].unsqueeze(2).to_broadcast([P, G, J]), ALU.subtract).then_inc(prep, 1)
            dve.wait_ge(weight_turned, 3)
            dve.tensor_copy(Wvp[:, :], pB[:, 0, 0:P]).then_inc(weight_copied, 1)
            dve.tensor_copy(global_part[:, :], pB[:, 0, P:P + 1]).then_inc(weight_copied, 1)
            dve.wait_ge(prep, 11)
            dve.wait_ge(zeroed, 1)

            def make_onehot(hot, cols, used, ready):
                wait_if(dve, sums_ready, used)
                dve.tensor_tensor(hot, over_tiles(window_iota[:, :]), over_window(cols),
                                  ALU.is_equal).then_inc(ready, 1)

            def split_residue(slot, edge_slot, loads, used):
                dve.wait_ge(edges_loaded[edge_slot], loads)
                wait_if(dve, sums_ready, used)
                dve.tensor_tensor(residue[slot], rows[:, edge_slot], upper(rows[:, edge_slot]), ALU.subtract) \
                    .then_inc(residue_ready, 1)

            def split_rest(slot, m, used):
                dve.wait_ge(residue_ready, m + 1)
                wait_if(dve, sums_ready, used)
                dve.tensor_tensor(lowest[slot][:, POOL_TILES:J], residue[slot][:, POOL_TILES:J],
                                  upper(residue[slot])[:, POOL_TILES:J], ALU.subtract).then_inc(lowest_rest_ready, 1)

            def add_sums(slot, base, n):
                dve.wait_ge(sums_ready, n + 1)
                wait_if(dve, sums_added, n)
                a = sums_norms[:, :, bass.ds(base, W)]
                dve.tensor_tensor(a, a, pA[:, slot, 0:2 * W].rearrange("p (s n) -> p s n", n=W), ALU.add) \
                    .then_inc(sums_added, 1)

            def group_cols(t, g):
                return t[:, bass.ds(g * J, J)]

            def edge_parts(i, g, loads):
                make_onehot(onehot16[i], group_cols(dst_w, g), g - RING + 1, onehot_ready)
                split_residue(i % 2, i, loads, g - 1)

            for g in range(RING):
                edge_parts(g, g, 16)
                if g >= 2:
                    add_sums(g % 2, load_base(dve, g - 2), g - 2)
                split_rest(g % 2, g, g - 1)
            with dve.Fori(1, G // RING) as k:
                for i in range(RING):
                    g = k * RING + i
                    edge_parts(i, g, (k + 1) * 16)
                    add_sums(i % 2, load_base(dve, g - 2), g - 2)
                    split_rest(i % 2, g, g - 1)
            for g in range(G - 2, G):
                add_sums(g % 2, load_base(dve, g), g)

            wide = load_wide(dve)

            def next_window(step_sem):
                dve.tensor_scalar(rel[:, :], rel[:, :], float(W), None, ALU.subtract).then_inc(step_sem, 1)

            with dve.If(wide > 0):
                dve.tensor_scalar(wide_f, dst_f[:, :], 1.0, None, ALU.add).then_inc(wide_step, 1)
                dve.wait_ge(wide_step, 1)
                dve.scalar_tensor_tensor(out=wide_f, in0=dst_w[:, :], scalar=float(W), in1=wide_f, op0=ALU.is_ge,
                                         op1=ALU.mult).then_inc(wide_step, 1)
                dve.wait_ge(wide_step, 2)
                dve.tensor_scalar(wide_f, wide_f, 1.0, None, ALU.subtract).then_inc(wide_step, 1)
                dve.wait_ge(wide_step, 3)
                with dve.Fori(0, G) as g:
                    split_residue(0, 0, (g + G // RING + 1) * 16, g * NW + WIDE)
                    split_rest(0, g + G, g * NW + WIDE)
                    dve.wait_ge(onehot_ready, g * NW + WIDE)
                    dve.tensor_copy(rel[:, :], group_cols(wide_f, g)).then_inc(wide_step, 1)
                    with dve.Fori(0, NW) as w:
                        n = g * NW + w + WIDE
                        dve.wait_ge(wide_step, g * (NW + 1) + w + 4)
                        make_onehot(onehot16[0], rel[:, :], n, onehot_ready)
                        dve.wait_ge(onehot_ready, n + 1)
                        next_window(wide_step)
                        add_sums(0, w * W, n)

            dve.wait_ge(x_loaded, 16)
            with dve.Fori(0, CHUNKS) as c:
                for t in range(CT):
                    dve.bn_stats(ln1[0][:, bass.ds(c * CT + t, 1), :].squeeze(1),
                                 X[:, bass.ds(c * CT + t, 1), :].squeeze(1)).then_inc(ln_step, 1)

            def ln_scale(tiles, turn, before, done):
                st, mean2, diff, var, r, sh = (t[:, :] if len(t.shape) == 2 else t for t in tiles)
                a, b = st[:, :, 1], st[:, :, 4]
                dve.wait_ge(ln_step, before)
                dve.tensor_tensor(mean2, a, b, ALU.add).then_inc(ln_step, 1)
                dve.tensor_tensor(diff, a, b, ALU.subtract).then_inc(ln_step, 1)
                dve.tensor_tensor(var, st[:, :, 2], st[:, :, 5], ALU.add).then_inc(ln_step, 1)
                dve.wait_ge(ln_step, before + 3)
                dve.tensor_tensor(diff, diff, diff, ALU.mult).then_inc(ln_step, 1)
                dve.wait_ge(ln_step, before + 4)
                dve.scalar_tensor_tensor(out=var, in0=diff, scalar=D / 4.0, in1=var,
                                         op0=ALU.mult, op1=ALU.add).then_inc(ln_step, 1)
                dve.wait_ge(ln_step, before + 5)
                dve.tensor_scalar(var, var, 1.0 / D, LN_EPS, ALU.mult, ALU.add).then_inc(var_ready, 1)
                dve.wait_ge(root_ready, turn)
                dve.tensor_tensor(diff, r, r, ALU.mult).then_inc(ln_step, 1)
                dve.wait_ge(ln_step, before + 6)
                dve.tensor_tensor(diff, diff, var, ALU.mult).then_inc(ln_step, 1)
                dve.wait_ge(ln_step, before + 7)
                dve.tensor_scalar(diff, diff, -0.5, 1.5, ALU.mult, ALU.add).then_inc(ln_step, 1)
                dve.wait_ge(ln_step, before + 8)
                dve.tensor_tensor(r, r, diff, ALU.mult).then_inc(ln_step, 1)
                dve.wait_ge(ln_step, before + LN_STEPS)
                dve.scalar_tensor_tensor(out=sh, in0=mean2, scalar=-0.5, in1=r,
                                         op0=ALU.mult, op1=ALU.mult).then_inc(done, 1)

            def invert_counts(c):
                a = norm[:, bass.ds(c * CN, CN)]
                dve.tensor_scalar(a, a, 1.0, None, ALU.max).then_inc(counts_bounded, 1)
                dve.wait_ge(counts_bounded, c + 1)
                dve.sem_inc(invert_turn, 1)
                dve.reciprocal(a, a).then_inc(inverse_ready, 1)

            def update_chunk(c, first=False, after=2):
                dve.wait_ge(softp_step, c * 2 + 1)
                dve.tensor_scalar(positive, two_banks(pB)[:, 0:CN], global_part[:, 0:1], 0.0, ALU.add, ALU.max) \
                    .then_inc(positive_ready, 1)
                if not first:
                    copy_h2T(c - 1)
                dve.wait_ge(softp_ready, c + 1)
                dve.wait_ge(positive_ready, c + 1)
                dve.tensor_tensor(softp, softp, positive, ALU.add).then_inc(softp_summed, 1)
                dve.wait_ge(softp_turned, c + 1)
                dve.wait_ge(stats_ready, 1)
                xc = X[:, bass.ds(c * CT, CT), :]
                dve.scalar_tensor_tensor(out=xc, in0=node_tiles(pA)[0:NT], scalar=-LN2, in1=xc,
                                         op0=ALU.add, op1=ALU.add).then_inc(x1_ready, 1)
                dve.wait_ge(stats_ready, 1)
                dve.wait_ge(x1_ready, c + 1)
                wait_if(dve, h2_ready, c)
                for t in range(CT):
                    dve.bn_stats(ln2[0][:, t, :], X[:, bass.ds(c * CT + t, 1), :].squeeze(1)).then_inc(ln_step, 1)
                ln_scale(ln2, c + 2, c * (CT + LN_STEPS) + TILES + LN_STEPS + CT, ln2_ready)
                if after >= 2:
                    invert_counts(c + 2)

            def copy_h2T(c):
                dve.wait_ge(h2_turned, c + 1)
                wait_if(dve, qk_ready, c)
                dve.tensor_copy(by_tile(h2T), node_tiles(pC, NT)).then_inc(h2T_ready, 1)

            ln_scale(ln1, 1, TILES, stats_ready)
            dve.wait_ge(sums_added, G)
            invert_counts(0)
            invert_counts(1)
            update_chunk(0, first=True)
            with dve.Fori(1, CHUNKS - 2) as c:
                update_chunk(c)
            update_chunk(CHUNKS - 2, after=1)
            update_chunk(CHUNKS - 1, after=0)
            copy_h2T(CHUNKS - 1)

            dve.wait_ge(cleared, 2)

            def make_mask(slot, cols, n, lag):
                wait_if(dve, probs_ready, n - lag + 1)
                dve.tensor_tensor(onehot[:, slot], over_tiles(window_iota[:, :]), over_window(cols),
                                  ALU.is_equal).then_inc(hot_ready, 1)
                dve.wait_ge(hot_ready, n + 1)
                wait_if(dve, masked_ready, n)
                dve.tensor_scalar(unmask, onehot[:, slot], 1.0, BIG, ALU.subtract, ALU.mult) \
                    .then_inc(unmask_ready, 1)

            def mask_scores(slot, n):
                dve.wait_ge(unmask_ready, n + 1)
                dve.wait_ge(scores_ready, n + 1)
                wait_if(dve, centred_ready, n)
                dve.tensor_tensor(masked, scores_ps[slot], unmask, ALU.add).then_inc(masked_ready, 1)
                dve.wait_ge(masked_ready, n + 1)
                wait_if(dve, top_turned, n)
                dve.tensor_reduce(tile_top[:, 0:W], masked.rearrange("p j n -> p n j"), AX.X, ALU.max) \
                    .then_inc(tile_top_ready, 1)

            def reduce_top(n):
                dve.wait_ge(top_turned, n + 1)
                wait_if(dve, top_spread, n)
                dve.tensor_reduce(group_top[:, :], turned_ps[0:W, :], AX.X, ALU.max).then_inc(group_top_ready, 1)

            def centre(base, n):
                dve.wait_ge(top_spread, n + 1)
                wait_if(dve, top_stored, n)
                wait_if(dve, centred_ready, n)
                window_top = top[:, bass.ds(base, W)]
                dve.tensor_tensor(new_top[:, :], window_top, spread_ps, ALU.max).then_inc(new_top_ready, 1)
                dve.wait_ge(new_top_ready, n + 1)
                wait_if(dve, rescale_ready, n)
                dve.tensor_tensor(drop[:, :], window_top, new_top[:, :], ALU.subtract).then_inc(drop_ready, 1)
                wait_if(dve, probs_ready, n)
                dve.tensor_tensor(centred, masked, over_tiles(new_top[:, :]), ALU.subtract) \
                    .then_inc(centred_ready, 1)
                dve.wait_ge(drop_ready, n + 1)
                dve.tensor_scalar(window_top, new_top[:, :], 0.0, None, ALU.add).then_inc(top_stored, 1)

            def weigh(slot, n):
                dve.wait_ge(exp_ready, n + 1)
                wait_if(dve, agg_ready, n)
                dve.scalar_tensor_tensor(out=probs, in0=centred, scalar=CLIP,
                                         in1=onehot[:, slot], op0=ALU.max, op1=ALU.mult).then_inc(probs_ready, 1)
                dve.wait_ge(probs_ready, n + 1)
                wait_if(dve, norm_added, n)
                dve.tensor_reduce(prob_sum[:, :], probs.rearrange("p j n -> p n j"), AX.X, ALU.add) \
                    .then_inc(prob_sum_ready, 1)

            def add_aggregate(slot, base, n):
                dve.wait_ge(rescale_ready, n + 1)
                wait_if(dve, norm_added, n)
                wait_if(dve, agg_added, n)
                a = sums_norms[:, :, bass.ds(base, W)]
                dve.tensor_tensor(a, a, rescale[:, slot:slot + 1].to_broadcast([P, 2, W]), ALU.mult) \
                    .then_inc(scaled, 1)
                a, s = acc[:, bass.ds(base, W)], norm[:, bass.ds(base, W)]
                dve.wait_ge(scaled, n + 1)
                dve.wait_ge(prob_sum_ready, n + 1)
                dve.tensor_tensor(s, s, prob_sum[:, :], ALU.add).then_inc(norm_added, 1)
                dve.wait_ge(agg_ready, n + 1)
                dve.tensor_tensor(a, a, agg_ps, ALU.add).then_inc(agg_added, 1)

            def edge_step(i, g, first=False, last=False):
                mask_scores(i, g)
                if not last:
                    make_mask(1 - i, group_cols(dst_w, g + 1), g + 1, 2)
                reduce_top(g)
                centre(load_base(dve, g), g)
                if not first:
                    add_aggregate(1 - i, load_base(dve, g - 1), g - 1)
                weigh(i, g)

            make_mask(0, group_cols(dst_w, 0), 0, 2)
            edge_step(0, 0, first=True)
            edge_step(1, 1)
            with dve.Fori(1, G // 2 - 1) as k:
                for i in range(2):
                    edge_step(i, k * 2 + i)
            edge_step(0, G - 2)
            edge_step(1, G - 1, last=True)
            add_aggregate(1, load_base(dve, G - 1), G - 1)
            with dve.If(wide > 0):
                with dve.Fori(0, G) as g:
                    dve.wait_ge(hot_ready, g * NW + WIDE)
                    dve.tensor_copy(rel[:, :], group_cols(wide_f, g)).then_inc(wide2_step, 1)
                    with dve.Fori(0, NW) as w:
                        n = g * NW + w + WIDE
                        dve.wait_ge(wide2_step, g * (NW + 1) + w + 1)
                        make_mask(0, rel[:, :], n, 1)
                        mask_scores(0, n)
                        next_window(wide2_step)
                        reduce_top(n)
                        centre(w * W, n)
                        weigh(0, n)
                        add_aggregate(0, w * W, n)
                dve.wait_ge(agg_added, WIDE + G * NW)
                dve.wait_ge(norm_added, WIDE + G * NW)

            def finish(slot, c, stored):
                dve.wait_ge(sum_mm, c + 1)
                dve.tensor_scalar(inverse[:, slot, :], pD[0:NT, slot, 0:CT], 1e-9, None, ALU.add) \
                    .then_inc(sum_bounded, 1)
                dve.wait_ge(sum_bounded, c + 1)
                dve.reciprocal(inverse[:, slot, :], inverse[:, slot, :]).then_inc(sum_inverted, 1)
                dve.wait_ge(sum_inverted, c + 1)
                dve.wait_ge(out_mm, c + 1)
                dve.wait_ge(bias_added, c + 1)
                wait_if(dve, out_stored[slot], stored)
                for t in range(CT):
                    dve.scalar_tensor_tensor(out=y[slot][:, t, :], in0=node_tiles((pB, pC)[slot])[0:NT, t, :],
                                             scalar=inverse[:, slot, t:t + 1], in1=h_in[slot][:, t, :],
                                             op0=ALU.mult, op1=ALU.add).then_inc(y_step, 1)
                dve.wait_ge(y_step, (c + 1) * CT)
                dve.wait_ge(all_added, 1)
                dve.scalar_tensor_tensor(out=y[slot], in0=y[slot], scalar=0.0, in1=X[:, bass.ds(c * CT, CT), :],
                                         op0=ALU.max, op1=ALU.add).then_inc(y_ready, 1)

            dve.wait_ge(agg_added, G)
            dve.wait_ge(norm_added, G)
            dve.sem_inc(all_added, 1)
            for i in range(2):
                finish(i, i, 0)
            with dve.Fori(1, CHUNKS // 2) as k:
                for i in range(2):
                    finish(i, k * 2 + i, k * 16)


_INS = ["x", "src", "dst", "edge_attr_128", "L0_gnn_global_feats", "L0_gnn_W", "L1_gnn_Wq", "L1_gnn_Wk",
        "L1_gnn_Wv", "L1_gnn_Wp", "L1_gnn_bp"]


def kernel(**inputs):
    import numpy as _np
    import concourse.bacc as _bacc
    from concourse import mybir as _mybir
    from concourse.bass_utils import run_bass_kernel_spmd as _run

    nc = _bacc.Bacc("TRN2", target_bir_lowering=False, num_devices=1)
    arrays, args = {}, []
    for name in _INS:
        a = _np.ascontiguousarray(inputs[name])
        arrays[f"in_{name}_dram"] = a
        args.append(nc.dram_tensor(f"in_{name}_dram", a.shape, _mybir.dt.from_np(a.dtype), kind="ExternalInput").ap())
    out = nc.dram_tensor("out_dram", inputs["x"].shape, F32, kind="ExternalOutput").ap()
    build(nc, *args, out)
    r = _run(nc, [arrays], core_ids=[0])
    return r.results[0]["out_dram"]
```

```python
from contextlib import ExitStack

import concourse.bass as bass
from concourse import mybir

F32 = mybir.dt.float32
BF16 = mybir.dt.bfloat16
I32 = mybir.dt.int32
ALU = mybir.AluOpType
ACT = mybir.ActivationFunctionType
AX = mybir.AxisListType

P = 128
J = 13
GROUP = P * J
W = 56
WS = 64
NT = 125
CT = 5
PAIR = 2
NODE_START = 6
POOL_TILES = 11
RING = 4
BIG = 1.0e30
CLIP = 1.9287498479639178e-22
LN_EPS = 1e-5
LN2 = 0.6931471805599453


def build(nc, x, src, dst, edge_attr, global_feats, W0, Wq, Wk, Wv, Wp, bp, out):
    N, D = x.shape
    E = src.shape[0]
    GF = global_feats.shape[1]
    assert D == P and N % (NT * CT) == 0
    G = -(-E // GROUP)
    LAST = E - GROUP
    REPEATED = (G - 1) * GROUP - LAST
    assert G % RING == 0 and G % 2 == 0 and 0 <= REPEATED < GROUP and G <= P
    TILES = N // NT
    CHUNKS = TILES // CT
    CN = CT * NT
    NW = -(-N // W)
    PAIRS = TILES // PAIR
    assert TILES % PAIR == 0 and NODE_START + PAIRS <= G // RING
    FIRST = 512
    NPAD = N + W
    SCALE = float(D) ** -0.5

    x_t = x.rearrange("(t p) d -> p t d", p=NT)
    out_t = out.rearrange("(t p) d -> p t d", p=NT)

    def group_edges(g):
        return edge_attr[bass.ds(g * GROUP, GROUP), :].rearrange("(p j) d -> p j d", j=J)

    def group_sources(g):
        return src[bass.ds(g * GROUP, GROUP)].rearrange("(p j) -> p j", j=J)

    with ExitStack() as ctx:
        def sb(name, shape, dt=F32):
            return ctx.enter_context(nc.sbuf_tensor(name, shape, dt))

        def ps(name, shape, dt=F32):
            return ctx.enter_context(nc.psum_tensor(name, shape, dt))

        def sem(name):
            return ctx.enter_context(nc.semaphore(name))

        h_table = nc.dram_tensor("h_table", [N, D], F32, kind="Internal").ap()
        h_table_t = h_table.rearrange("(t p) d -> p t d", p=NT)

        ident = sb("ident", [P, P])
        ones = sb("ones", [P, P])
        ones16 = sb("ones16", [P, P], BF16)
        window_iota = sb("window_iota", [P, W])
        WnT = sb("WnT", [P, P])
        WeT = sb("WeT", [P, P])
        WgT = sb("WgT", [GF, P])
        WpT = sb("WpT", [P, P])
        Wqk = sb("Wqk", [P, P])
        Wvp = sb("Wvp", [P, P])
        g0 = sb("g0", [GF, 1])
        global_part = sb("global_part", [P, 1])
        bp_rep = sb("bp_rep", [NT, P])

        dst_f = sb("dst_f", [P, G * J])
        dst_w = sb("dst_w", [P, G * J])
        wide_f = dst_f[:, :]
        rel = sb("rel", [P, J])
        low_p = sb("low_p", [P, G])
        high_p = sb("high_p", [P, G])
        low = sb("low", [G, 1])
        high = sb("high", [G, 1])
        low_diag = sb("low_diag", [G, G])
        base_i = sb("base_i", [1, G], I32)
        span_row = sb("span_row", [1, G])
        widest = sb("widest", [1, 1])
        wide_i = sb("wide_i", [1, 1], I32)

        X = sb("X", [NT, TILES, D])
        sums_norms = sb("sums_norms", [P, 2, NPAD])
        acc = sums_norms[:, 0, :]
        norm = sums_norms[:, 1, :]
        top = sb("top", [P, NPAD])
        QK = sb("QK", [P, NPAD])

        dst_i = QK[:, 0:G * J].bitcast(I32)
        W0_sb = QK[:, G * J:G * J + 2 * D + GF]
        Wq_sb, Wk_sb, Wv_sb, Wp_sb = (QK[:, N - (i + 1) * P:N - i * P] for i in range(4))

        rows = sb("rows", [P, RING, J, D])
        srcs = sb("srcs", [P, RING, J], I32)

        work = sb("work", [P, 4 * J * P])
        residue = [work[:, i * J * D:(i + 1) * J * D].rearrange("p (j d) -> p j d", d=D) for i in range(2)]
        lowest = [work[:, (4 + i) * J * D // 2:(5 + i) * J * D // 2].bitcast(BF16)
                  .rearrange("p (j d) -> p j d", d=D) for i in range(2)]
        onehot16 = [work[:, 3 * J * D + i * J * W // 2:3 * J * D + (i + 1) * J * W // 2].bitcast(BF16)
                    .rearrange("p (j n) -> p j n", n=W) for i in range(RING)]

        def upper(t):
            return t.bitcast(BF16)[:, :, 1:2 * D:2]

        rowsT = work[:, 0:J * P].rearrange("p (j e) -> p j e", e=P)
        unmask, masked, centred, probs = (
            work[:, J * P + i * J * W:J * P + (i + 1) * J * W].rearrange("p (j n) -> p j n", n=W)
            for i in range(4))
        onehot = sb("onehot", [P, 2, J, W])
        tile_top = sb("tile_top", [P, W])
        group_top = sb("group_top", [W, 1])
        prob_sum = sb("prob_sum", [P, W])
        new_top = sb("new_top", [P, W])
        drop = sb("drop", [P, W])
        inverse = sb("inverse", [NT, 2, CT])
        rescale = sb("rescale", [P, 2, W])

        sum1, negmean1, squares1, var1, rstd1, newton1, shift1 = (
            sb(f"ln1_{what}", [NT, TILES]) for what in
            ("sum", "negmean", "squares", "var", "rstd", "newton", "shift"))
        stats2 = sb("ln2_stats", [NT, CT, 6])
        mean2, diff2, var2, rstd2, newton2, shift2 = (
            sb(f"ln2_{what}", [NT, CT]) for what in ("mean", "diff", "var", "rstd", "newton", "shift"))

        def chunk_buffer(slot, half, parts=P):
            return rows[0:parts, slot].rearrange("p j d -> p (j d)")[:, half * 6 * D:half * 6 * D + CT * D]\
                .rearrange("p (t d) -> p t d", d=D)

        def flat(chunk):
            return chunk.rearrange("p t d -> p (t d)")[:, 0:CN]

        def by_tile(flat_chunk):
            return flat_chunk.rearrange("p (t n) -> p t n", n=NT)

        meanT = flat(chunk_buffer(0, 0))
        part_mean = flat(chunk_buffer(0, 1))
        updateT = flat(chunk_buffer(1, 0))
        softp = flat(chunk_buffer(1, 1))
        h2 = chunk_buffer(2, 0, NT)
        h2T = flat(chunk_buffer(2, 1))
        log_count = flat(chunk_buffer(3, 0))
        inverse_count = flat(chunk_buffer(3, 1))
        correction = work[:, 0:CN]
        spare = onehot[:, :, :, :].rearrange("p s j n -> p (s j n)")
        h1 = spare[0:NT, 0:PAIR * D].rearrange("p (t d) -> p t d", d=D)
        h1T = spare[:, PAIR * D:PAIR * D + PAIR * NT]
        unused = spare[0:NT, 3 * PAIR * D:(3 * PAIR + CT) * D].rearrange("p (t d) -> p t d", d=D)
        agg_sumT = [rows[:, i].rearrange("p j d -> p (j d)")[:, 0:2 * CN].rearrange("p (s n) -> p s n", n=CN)
                    for i in range(2)]
        h_in = [chunk_buffer(2, 0, NT), chunk_buffer(2, 1, NT)]
        y = [chunk_buffer(3, 0, NT), chunk_buffer(3, 1, NT)]

        pA = ps("pA", [P, 2, 512])
        pB = ps("pB", [P, 2, 512])
        pC = ps("pC", [P, 2, 512])
        pD = ps("pD", [P, 2, 512])

        def two_banks(t):
            return t[:, :, :].rearrange("p b n -> p (b n)")

        def node_tiles(t, width=P):
            return two_banks(t)[:, 0:CT * P].rearrange("p (t d) -> p t d", d=P)[:, :, 0:width]

        scores_ps = [two_banks(t)[:, 0:J * WS].rearrange("p (j n) -> p j n", n=WS)[:, :, 0:W] for t in (pB, pC)]
        turned_ps = pD[0:W, 0, 0:P]
        spread_ps = pD[:, 0, P:P + W]
        agg_ps = pD[:, 1, 0:W]

        dst_loaded = sem("dst_loaded")
        x_loaded = sem("x_loaded")
        weights_loaded = sem("weights_loaded")
        edges_loaded = [sem(f"edges_loaded{i}") for i in range(RING)]
        const_made = sem("const_made")
        zeroed = sem("zeroed")
        weight_turned = sem("weight_turned")
        weight_copied = sem("weight_copied")
        prep = sem("prep")
        bounds_turned = sem("bounds_turned")
        repeated_masked = sem("repeated_masked")
        base_ready = sem("base_ready")

        onehot_ready = sem("onehot_ready")
        residue_ready = sem("residue_ready")
        lowest_ready = sem("lowest_ready")
        lowest_rest_ready = sem("lowest_rest_ready")
        sums_ready = sem("sums_ready")
        sums_added = sem("sums_added")
        wide_step = sem("wide_step")

        tile_sums_ready = sem("tile_sums_ready")
        mean1_ready = sem("mean1_ready")
        sums_turn = sem("sums_turn")
        squares_ready = sem("squares_ready")
        ln_step = sem("ln_step")
        newton_step = sem("newton_step")
        stats_ready = sem("stats_ready")
        var_ready = sem("var_ready")
        log_ready = sem("log_ready")
        root_ready = sem("root_ready")
        h1_ready = sem("h1_ready")
        h1_turned = sem("h1_turned")
        h1T_ready = sem("h1T_ready")
        node_part_ready = sem("node_part_ready")
        node_part_turn = sem("node_part_turn")
        node_part_stored = sem("node_part_stored")
        counts_bounded = sem("counts_bounded")
        log_count_turn = sem("log_count_turn")
        log_count_ready = sem("log_count_ready")
        inverse_ready = sem("inverse_ready")
        inverse_used = sem("inverse_used")
        mean_turn = sem("mean_turn")
        correction_step = sem("correction_step")
        mean_ready = sem("mean_ready")
        update_mm = sem("update_mm")
        update_ready = sem("update_ready")
        softp_step = sem("softp_step")
        softp_ready = sem("softp_ready")
        softp_summed = sem("softp_summed")
        softp_turned = sem("softp_turned")
        x1_ready = sem("x1_ready")
        ln2_ready = sem("ln2_ready")
        h2_turn = sem("h2_turn")
        h2_ready = sem("h2_ready")
        h2_stored = sem("h2_stored")
        h2_turned = sem("h2_turned")
        h2T_ready = sem("h2T_ready")
        qk_ready = sem("qk_ready")
        qk_stored = sem("qk_stored")

        cleared = sem("cleared")
        qk_padded = sem("qk_padded")
        srcs_loaded = [sem(f"srcs_loaded{i}") for i in range(RING)]
        gather_turn = sem("gather_turn")
        gathered = [sem(f"gathered{i}") for i in range(RING)]
        rows_turned = sem("rows_turned")
        rowsT_ready = sem("rowsT_ready")
        scores_ready = sem("scores_ready")
        hot_ready = sem("hot_ready")
        unmask_ready = sem("unmask_ready")
        masked_ready = sem("masked_ready")
        tile_top_ready = sem("tile_top_ready")
        top_turn = sem("top_turn")
        top_turned = sem("top_turned")
        group_top_ready = sem("group_top_ready")
        top_spread = sem("top_spread")
        new_top_ready = sem("new_top_ready")
        drop_ready = sem("drop_ready")
        rescale_ready = sem("rescale_ready")
        top_stored = sem("top_stored")
        centred_ready = sem("centred_ready")
        exp_ready = sem("exp_ready")
        probs_ready = sem("probs_ready")
        prob_sum_ready = sem("prob_sum_ready")
        agg_ready = sem("agg_ready")
        scaled = sem("scaled")
        agg_added = sem("agg_added")
        wide2_step = sem("wide2_step")

        norm_added = sem("norm_added")
        all_added = sem("all_added")
        sum_mm = sem("sum_mm")
        sum_bounded = sem("sum_bounded")
        sum_inverted = sem("sum_inverted")
        aggT_ready = sem("aggT_ready")
        bias_added = sem("bias_added")
        h_in_loaded = [sem(f"h_in_loaded{i}") for i in range(2)]
        out_mm = sem("out_mm")
        y_step = sem("y_step")
        y_ready = sem("y_ready")
        out_stored = [sem(f"out_stored{i}") for i in range(2)]

        GATHER = 16 * J
        WIDE = G

        def wait_if(eng, s, value):
            if not isinstance(value, int) or value > 0:
                eng.wait_ge(s, value)

        def over_tiles(row, n=W):
            return row.unsqueeze(1).to_broadcast([P, J, n])

        def over_window(cols):
            return cols.unsqueeze(2).to_broadcast([P, J, W])

        def load_base(eng, g):
            return eng.value_load(base_i[0:1, bass.ds(g, 1)], min_val=0, max_val=N - 1)

        def load_wide(eng):
            return eng.value_load(wide_i[0:1, 0:1], min_val=0, max_val=1)

        block = ctx.enter_context(nc.Block())

        @block.sync
        def _(sp):
            sp.dma_start(dst_i[:, 0:(G - 1) * J].rearrange("p (g j) -> p g j", j=J),
                         dst[0:(G - 1) * GROUP].rearrange("(g p j) -> p g j", p=P, j=J)).then_inc(dst_loaded, 16)
            sp.dma_start(dst_i[:, (G - 1) * J:G * J],
                         dst[LAST:E].rearrange("(p j) -> p j", j=J)).then_inc(dst_loaded, 16)
            for tile, source in ((W0_sb, W0), (Wq_sb, Wq), (Wk_sb, Wk), (Wv_sb, Wv), (Wp_sb, Wp)):
                sp.dma_start(tile[:, :], source).then_inc(weights_loaded, 16)
            sp.dma_start(bp_rep[:, :], bp.unsqueeze(0).to_broadcast([NT, P])).then_inc(weights_loaded, 16)
            sp.dma_start(g0[:, :], global_feats[0:1, :].rearrange("a f -> f a")).then_inc(weights_loaded, 16)
            sp.dma_start(X[:, :, :], x_t).then_inc(x_loaded, 16)

            def load_edges(source, slot, free):
                wait_if(sp, sums_ready, free)
                sp.dma_start(rows[:, slot], source).then_inc(edges_loaded[slot], 16)

            for g in range(RING):
                load_edges(group_edges(g), g, 0)
            with sp.Fori(1, G // RING - 1) as k:
                for i in range(RING):
                    load_edges(group_edges(k * RING + i), i, k * RING + (i - RING + 1))
            for g in range(G - RING, G - 1):
                load_edges(group_edges(g), g % RING, g - RING + 1)
            last_edges = edge_attr[LAST:E, :].rearrange("(p j) d -> p j d", j=J)
            load_edges(last_edges, (G - 1) % RING, G - RING)

            sp.wait_ge(base_ready, 1)
            wide = load_wide(sp)
            with sp.If(wide > 0):
                with sp.Fori(0, G - 1) as g:
                    load_edges(group_edges(g), 0, WIDE + g * NW)
                load_edges(last_edges, 0, WIDE + (G - 1) * NW)

            with sp.Fori(0, CHUNKS) as c:
                sp.wait_ge(h2_ready, c + 1)
                sp.dma_start(h_table_t[:, bass.ds(c * CT, CT), :], h2).then_inc(h2_stored, 16)

            def load_sources(source, slot, engine_done):
                for s, value in engine_done:
                    wait_if(sp, s, value)
                sp.dma_start(srcs[:, slot], source).then_inc(srcs_loaded[slot], 16)

            for g in range(RING):
                load_sources(group_sources(g), g, [])
            with sp.Fori(1, G // RING - 1) as k:
                for i in range(RING):
                    load_sources(group_sources(k * RING + i), i, [(gathered[i], k * GATHER)])
            for g in range(G - RING, G - 1):
                load_sources(group_sources(g), g % RING, [(gathered[g % RING], g // RING * GATHER)])
            last_sources = src[LAST:E].rearrange("(p j) -> p j", j=J)
            load_sources(last_sources, (G - 1) % RING, [(gathered[(G - 1) % RING], (G // RING - 1) * GATHER)])
            with sp.If(wide > 0):
                with sp.Fori(0, G - 1) as g:
                    load_sources(group_sources(g), 0, [(gathered[0], (g + G // RING) * GATHER)])
                load_sources(last_sources, 0, [(gathered[0], (G - 1 + G // RING) * GATHER)])

            def load_h(c, slot):
                sp.dma_start(h_in[slot], h_table_t[:, bass.ds(c * CT, CT), :]).then_inc(h_in_loaded[slot], 16)

            def store_y(c, slot):
                sp.wait_ge(y_ready, c + 1)
                sp.dma_start(out_t[:, bass.ds(c * CT, CT), :], y[slot]).then_inc(out_stored[slot], 16)

            sp.wait_ge(all_added, 1)
            load_h(0, 0)
            load_h(1, 1)
            with sp.Fori(0, CHUNKS // 2 - 1) as k:
                for i in range(2):
                    store_y(k * 2 + i, i)
                    load_h(k * 2 + i + 2, i)
            for i in range(2):
                store_y(CHUNKS - 2 + i, i)
            for i in range(2):
                sp.wait_ge(out_stored[i], 16 * (CHUNKS // 2))

        @block.gpsimd
        def _(pool):
            pool.memset(ident[:, :], 0.0).then_inc(const_made, 1)
            pool.memset(ones[:, :], 1.0).then_inc(const_made, 1)
            pool.memset(ones16[:, :], 1.0).then_inc(const_made, 1)
            pool.iota(window_iota[:, :], pattern=[[1, W]], base=0, channel_multiplier=0,
                      allow_small_or_imprecise_dtypes=True).then_inc(const_made, 1)
            pool.wait_ge(const_made, 4)
            pool.affine_select(out=ident[:, :], in_=ident[:, :], compare_op=ALU.not_equal, fill=1.0, base=0,
                               pattern=[[-1, P]], channel_multiplier=1).then_inc(const_made, 1)
            pool.memset(sums_norms[:, :, :], 0.0).then_inc(zeroed, 1)
            pool.wait_ge(prep, 3)
            pool.affine_select(out=dst_f[:, (G - 1) * J:G * J], in_=dst_f[:, (G - 1) * J:G * J],
                               compare_op=ALU.is_ge, fill=-1.0, base=-REPEATED, pattern=[[1, J]],
                               channel_multiplier=J).then_inc(repeated_masked, 1)
            pool.memset(QK[:, N:NPAD], 0.0).then_inc(qk_padded, 1)

            def split_lowest(slot, m, used):
                pool.wait_ge(residue_ready, m + 1)
                wait_if(pool, sums_ready, used)
                pool.tensor_tensor(lowest[slot][:, 0:POOL_TILES], residue[slot][:, 0:POOL_TILES],
                                   upper(residue[slot])[:, 0:POOL_TILES], ALU.subtract) \
                    .then_inc(lowest_ready, 1)

            split_lowest(0, 0, 0)
            split_lowest(1, 1, 0)
            with pool.Fori(1, G // 2) as k:
                for i in range(2):
                    split_lowest(i, k * 2 + i, k * 2 + i - 1)
            pool.wait_ge(base_ready, 1)
            wide = load_wide(pool)
            with pool.If(wide > 0):
                with pool.Fori(0, G) as g:
                    split_lowest(0, g + G, g * NW + WIDE)

            def mean_features(c):
                pool.wait_ge(inverse_ready, c + 1)
                wait_if(pool, mean_ready, c)
                pool.sem_inc(mean_turn, 1)
                pool.tensor_tensor(correction, norm[:, bass.ds(c * CN, CN)], inverse_count, ALU.mult) \
                    .then_inc(correction_step, 1)
                pool.tensor_tensor(part_mean, acc[:, bass.ds(c * CN, CN)], inverse_count, ALU.mult) \
                    .then_inc(inverse_used, 1)
                pool.wait_ge(correction_step, c * 2 + 1)
                pool.sem_inc(mean_turn, 1)
                pool.tensor_scalar(correction, correction, -1.0, 2.0, ALU.mult, ALU.add) \
                    .then_inc(correction_step, 1)
                pool.wait_ge(correction_step, c * 2 + 2)
                pool.wait_ge(inverse_used, c + 1)
                wait_if(pool, update_mm, c)
                pool.tensor_tensor(meanT, part_mean, correction, ALU.mult).then_inc(mean_ready, 1)

            mean_features(0)
            with pool.Fori(1, CHUNKS) as c:
                mean_features(c)

            pool.wait_ge(update_ready, CHUNKS)
            pool.memset(top[:, :], -BIG).then_inc(cleared, 1)
            pool.memset(sums_norms[:, :, :], 0.0).then_inc(cleared, 1)

            last_row = pool.to_reg(N - 1)

            def gather(slot, loads, free):
                pool.wait_ge(srcs_loaded[slot], loads)
                wait_if(pool, agg_ready, free)
                pool.sem_inc(gather_turn, 1)
                for j in range(J):
                    pool.indirect_dma_start(
                        out=rows[:, slot, j, :], out_offset=None, in_=h_table,
                        in_offset=bass.IndirectOffsetOnAxis(ap=srcs[:, slot, j:j + 1], axis=0),
                        bounds_check=last_row).then_inc(gathered[slot], 16)

            pool.wait_ge(h2_stored, 16 * CHUNKS)
            pool.wait_ge(x1_ready, CHUNKS)
            gather(0, 16, 0)
            gather(1, 16, 0)
            pool.wait_ge(qk_ready, CHUNKS)
            gather(2, 16, 0)
            gather(3, 16, 0)
            with pool.Fori(1, G // RING) as k:
                for i in range(RING):
                    gather(i, (k + 1) * 16, k * RING + (i - RING + 1))
            with pool.If(wide > 0):
                with pool.Fori(0, G) as g:
                    gather(0, (g + G // RING + 1) * 16, WIDE + g * NW)

            def add_bias(slot, c, loads):
                pool.wait_ge(h_in_loaded[slot], loads)
                pool.tensor_tensor(h_in[slot], h_in[slot], bp_rep[:, :].unsqueeze(1).to_broadcast([NT, CT, P]),
                                   ALU.add).then_inc(bias_added, 1)

            for i in range(2):
                add_bias(i, i, 16)
            with pool.Fori(1, CHUNKS // 2) as k:
                for i in range(2):
                    add_bias(i, k * 2 + i, (k + 1) * 16)

        @block.tensor
        def _(pe):
            pe.wait_ge(const_made, 5)
            pe.wait_ge(weights_loaded, 16 * 7)
            pe.transpose(pA[:, 0, 0:P], W0_sb[:, 0:D], ident[:, :])
            pe.transpose(pA[:, 0, P:2 * P], W0_sb[:, D:2 * D], ident[:, :])
            pe.transpose(pA[0:GF, 0, 2 * P:3 * P], W0_sb[:, 2 * D:2 * D + GF], ident[:, :])
            pe.transpose(pA[:, 0, 3 * P:4 * P], Wp_sb[:, :], ident[:, :]).then_inc(weight_turned, 1)
            pe.matmul(pA[:, 1, 0:P], Wq_sb[:, :], Wk_sb[:, :], start=True, stop=True).then_inc(weight_turned, 1)
            pe.wait_ge(weight_copied, 4)
            pe.matmul(pB[:, 0, 0:P], Wv_sb[:, :], WpT[:, :], start=True, stop=True)
            pe.matmul(pB[:, 0, P:P + 1], WgT[:, :], g0[:, :], start=True, stop=True).then_inc(weight_turned, 1)

            pe.wait_ge(prep, 3)
            pe.transpose(pD[0:G, 0, 0:P], low_p[:, :], ident[:, :])
            pe.transpose(pD[0:G, 0, P:2 * P], high_p[:, :], ident[:, :]).then_inc(bounds_turned, 1)
            pe.wait_ge(prep, 6)
            pe.matmul(pD[:, 1, 0:G], ones[0:G, :], low_diag[:, :], start=True, stop=True).then_inc(bounds_turned, 1)
            pe.transpose(pD[0:1, 1, P:P + G], high[:, :], ident[0:G, 0:G]).then_inc(bounds_turned, 1)

            def sums(slot, edge_slot, hot, loads, n, m, lag):
                pe.wait_ge(edges_loaded[edge_slot], loads)
                pe.wait_ge(onehot_ready, n + 1)
                wait_if(pe, sums_added, n - lag + 1)
                for j in range(J):
                    pe.matmul(pA[:, slot, W:2 * W], ones16[:, :], hot[:, j, :], start=(j == 0), stop=(j == J - 1))
                for j in range(J):
                    pe.matmul(pA[:, slot, 0:W], upper(rows[:, edge_slot])[:, j, :], hot[:, j, :],
                              start=(j == 0), stop=False)
                pe.wait_ge(residue_ready, m + 1)
                for j in range(J):
                    pe.matmul(pA[:, slot, 0:W], upper(residue[slot])[:, j, :], hot[:, j, :], start=False, stop=False)
                pe.wait_ge(lowest_ready, m + 1)
                pe.wait_ge(lowest_rest_ready, m + 1)
                for j in range(J):
                    mm = pe.matmul(pA[:, slot, 0:W], lowest[slot][:, j, :], hot[:, j, :],
                                   start=False, stop=(j == J - 1))
                mm.then_inc(sums_ready, 1)

            def turn_h1(p):
                pe.wait_ge(h1_ready, p + 1)
                wait_if(pe, h1T_ready, p)
                for t in range(PAIR):
                    mm = pe.transpose(pC[:, 0, t * P:t * P + NT], h1[:, t, :], ident[0:NT, 0:NT])
                mm.then_inc(h1_turned, 1)

            def project_nodes(p):
                pe.wait_ge(h1T_ready, p + 1)
                wait_if(pe, node_part_stored, p)
                pe.matmul(pD[:, 0, 0:PAIR * NT], WnT[:, :], h1T, start=True, stop=True) \
                    .then_inc(node_part_ready, 1)

            def edge_round(k, pair=None):
                for i in range(RING):
                    sums(i % 2, i, onehot16[i], (k + 1) * 16, k * RING + i, k * RING + i, 2)
                    if pair is not None and i == 0:
                        turn_h1(pair)
                    if pair is not None and i == 2:
                        project_nodes(pair)

            pe.wait_ge(weight_copied, 7)
            edge_round(0)
            with pe.Fori(1, NODE_START) as k:
                edge_round(k)
            edge_round(NODE_START, 0)
            with pe.Fori(1, PAIRS) as p:
                edge_round(p + NODE_START, p)
            for k in range(NODE_START + PAIRS, G // RING):
                edge_round(k)
            pe.wait_ge(base_ready, 1)
            wide = load_wide(pe)
            with pe.If(wide > 0):
                with pe.Fori(0, G) as g:
                    with pe.Fori(0, NW) as w:
                        sums(0, 0, onehot16[0], (g + G // RING + 1) * 16, g * NW + w + WIDE, g + G, 1)

            def project_mean(c):
                pe.wait_ge(mean_ready, c + 1)
                wait_if(pe, update_ready, c)
                pe.matmul(pB[:, 0, 0:FIRST], WeT[:, :], meanT[:, 0:FIRST], start=True, stop=True)
                pe.matmul(pB[:, 1, 0:CN - FIRST], WeT[:, :], meanT[:, FIRST:CN],
                          start=True, stop=True).then_inc(update_mm, 1)

            def turn_update(c):
                pe.wait_ge(softp_summed, c + 1)
                wait_if(pe, x1_ready, c)
                for t in range(CT):
                    mm = pe.transpose(node_tiles(pA)[0:NT, t, :], by_tile(softp)[:, t, :], ident[:, :])
                mm.then_inc(softp_turned, 1)

            def query(c):
                pe.wait_ge(h2_ready, c + 1)
                wait_if(pe, h2T_ready, c)
                for t in range(CT):
                    mm = pe.transpose(node_tiles(pC, NT)[:, t, :], h2[:, t, :], ident[0:NT, 0:NT])
                mm.then_inc(h2_turned, 1)
                pe.wait_ge(h2T_ready, c + 1)
                wait_if(pe, qk_stored, c)
                pe.matmul(pD[:, 0, 0:FIRST], Wqk[:, :], h2T[:, 0:FIRST], start=True, stop=True)
                pe.matmul(pD[:, 1, 0:CN - FIRST], Wqk[:, :], h2T[:, FIRST:CN],
                          start=True, stop=True).then_inc(qk_ready, 1)

            pe.wait_ge(sums_added, G)
            pe.wait_ge(node_part_stored, PAIRS)
            project_mean(0)
            turn_update(0)
            project_mean(1)
            turn_update(1)
            project_mean(2)
            query(0)
            with pe.Fori(2, CHUNKS - 1) as c:
                turn_update(c)
                project_mean(c + 1)
                query(c - 1)
            turn_update(CHUNKS - 1)
            query(CHUNKS - 2)
            query(CHUNKS - 1)

            pe.wait_ge(qk_stored, CHUNKS)
            pe.wait_ge(qk_padded, 1)
            TURNS = [range(0, 4), range(4, 7), range(7, 10), range(10, 13)]

            def turn_rows(rows_slot, gathers, m, turns):
                if turns[0] == 0:
                    pe.wait_ge(gathered[rows_slot], gathers)
                for q in turns:
                    wait_if(pe, rowsT_ready, m * 4 + q - 1)
                    for a, j in enumerate(TURNS[q]):
                        mm = pe.transpose(pA[:, q % 2, a * P:(a + 1) * P], rows[:, rows_slot, j, :], ident[:, :])
                    mm.then_inc(rows_turned, 1)

            def scores(slot, base, n, m, lag):
                pe.wait_ge(rowsT_ready, m * 4 + 4)
                wait_if(pe, masked_ready, n - lag + 1)
                for j in range(J):
                    mm = pe.matmul(scores_ps[slot][:, j, :], rowsT[:, j, :], QK[:, bass.ds(base, W)],
                                   start=True, stop=True)
                mm.then_inc(scores_ready, 1)

            def turn_top(n):
                pe.wait_ge(tile_top_ready, n + 1)
                wait_if(pe, new_top_ready, n)
                pe.sem_inc(top_turn, 1)
                pe.transpose(turned_ps, tile_top[:, :], ident[:, :]).then_inc(top_turned, 1)

            def spread_top(n):
                pe.wait_ge(const_made, 5)
                pe.wait_ge(group_top_ready, n + 1)
                pe.transpose(spread_ps, group_top[:, :].to_broadcast([W, P]), ident[0:W, 0:W]) \
                    .then_inc(top_spread, 1)

            def aggregate(rows_slot, n, tiles):
                if tiles[0] == 0:
                    pe.wait_ge(probs_ready, n + 1)
                    wait_if(pe, agg_added, n)
                for j in tiles:
                    mm = pe.matmul(agg_ps, rows[:, rows_slot, j, :], probs[:, j, :],
                                   start=(j == 0), stop=(j == J - 1))
                if tiles[-1] == J - 1:
                    mm.then_inc(agg_ready, 1)

            ALL, EARLY, LATE = range(J), range(0, 6), range(6, J)

            def edge_step(i, g, next_gathers, first=False, last=False):
                scores(i % 2, load_base(pe, g), g, g, 2)
                if not last:
                    turn_rows((i + 1) % RING, next_gathers, g + 1, (0, 1))
                if not first:
                    aggregate((i - 1) % RING, g - 1, EARLY)
                if not last:
                    turn_rows((i + 1) % RING, next_gathers, g + 1, (2, 3))
                turn_top(g)
                if not first:
                    aggregate((i - 1) % RING, g - 1, LATE)
                spread_top(g)

            turn_rows(0, GATHER, 0, (0, 1, 2, 3))
            for g in range(RING):
                edge_step(g, g, (2 if g == RING - 1 else 1) * GATHER, first=(g == 0))
            with pe.Fori(1, G // RING - 1) as k:
                for i in range(RING):
                    edge_step(i, k * RING + i, (k + (2 if i == RING - 1 else 1)) * GATHER)
            for i in range(RING):
                edge_step(i, G - RING + i, G // RING * GATHER, last=(i == RING - 1))
            aggregate((G - 1) % RING, G - 1, ALL)
            with pe.If(wide > 0):
                with pe.Fori(0, G) as g:
                    turn_rows(0, (g + G // RING + 1) * GATHER, g + G, (0, 1, 2, 3))
                    with pe.Fori(0, NW) as w:
                        n = g * NW + w + WIDE
                        scores(0, w * W, n, g + G, 1)
                        turn_top(n)
                        spread_top(n)
                        aggregate(0, n, ALL)

            def project_aggregate(i, c):
                pe.wait_ge(aggT_ready, c + 1)
                wait_if(pe, y_step, (c - 1) * CT)
                for t in range(CT):
                    mm = pe.matmul(pD[0:NT, i, t:t + 1], by_tile(agg_sumT[i][:, 1, :])[:, t, :], ones[:, 0:1],
                                   start=True, stop=True)
                mm.then_inc(sum_mm, 1)
                for t in range(CT):
                    mm = pe.matmul(node_tiles((pB, pC)[i])[0:NT, t, :], by_tile(agg_sumT[i][:, 0, :])[:, t, :],
                                   Wvp[:, :], start=True, stop=True)
                mm.then_inc(out_mm, 1)

            for i in range(2):
                project_aggregate(i, i)
            with pe.Fori(1, CHUNKS // 2) as k:
                for i in range(2):
                    project_aggregate(i, k * 2 + i)

        @block.scalar
        def _(act):
            def root(v, r, turn):
                act.wait_ge(var_ready, turn)
                act.activation(r[:, :], v[:, :], ACT.Ln).then_inc(log_ready, 1)
                act.wait_ge(log_ready, turn)
                act.activation(r[:, :], r[:, :], ACT.Exp, scale=-0.5).then_inc(root_ready, 1)

            act.preload_act_table_set("natural_log_exp_and_others")

            act.wait_ge(x_loaded, 16)
            def tile_sums(c):
                if not isinstance(c, int):
                    act.wait_ge(tile_sums_ready, c * CT)
                    act.sem_inc(sums_turn, 1)
                for t in range(CT):
                    act.activation(unused[:, t, :], X[:, bass.ds(c * CT + t, 1), :].squeeze(1), ACT.Copy,
                                   accum_out=sum1[:, bass.ds(c * CT + t, 1)]).then_inc(tile_sums_ready, 1)

            tile_sums(0)
            with act.Fori(1, CHUNKS) as c:
                tile_sums(c)
            act.wait_ge(tile_sums_ready, TILES)
            act.activation(negmean1[:, :], sum1[:, :], ACT.Copy, scale=-1.0 / D).then_inc(mean1_ready, 1)
            act.wait_ge(mean1_ready, 1)
            def tile_squares(c):
                if not isinstance(c, int):
                    act.wait_ge(squares_ready, c * CT)
                    act.sem_inc(sums_turn, 1)
                for t in range(CT):
                    act.activation(unused[:, t, :], X[:, bass.ds(c * CT + t, 1), :].squeeze(1), ACT.Square,
                                   bias=negmean1[:, bass.ds(c * CT + t, 1)],
                                   accum_out=squares1[:, bass.ds(c * CT + t, 1)]).then_inc(squares_ready, 1)

            tile_squares(0)
            with act.Fori(1, CHUNKS) as c:
                tile_squares(c)
            root(var1, rstd1, 1)

            def node_part(p):
                wait_if(act, h1_turned, p)
                act.wait_ge(stats_ready, 1)
                for t in range(PAIR):
                    a = act.activation(h1[:, t, :], X[:, bass.ds(p * PAIR + t, 1), :].squeeze(1), ACT.Relu,
                                       bias=shift1[:, bass.ds(p * PAIR + t, 1)],
                                       scale=rstd1[:, bass.ds(p * PAIR + t, 1)])
                a.then_inc(h1_ready, 1)
                act.wait_ge(h1_turned, p + 1)
                wait_if(act, node_part_ready, p)
                act.activation(h1T.rearrange("p (t n) -> p t n", n=NT),
                               pC[:, 0, 0:PAIR * P].rearrange("p (t n) -> p t n", n=P)[:, :, 0:NT],
                               ACT.Copy).then_inc(h1T_ready, 1)
                act.wait_ge(node_part_ready, p + 1)
                act.sem_inc(node_part_turn, 1)
                act.activation(top[:, bass.ds(p * PAIR * NT, PAIR * NT)], pD[:, 0, 0:PAIR * NT], ACT.Identity,
                               bias=global_part[:, 0:1]).then_inc(node_part_stored, 1)

            act.wait_ge(weight_copied, 7)
            node_part(0)
            with act.Fori(1, PAIRS) as p:
                node_part(p)

            act.wait_ge(base_ready, 1)
            wide = load_wide(act)

            def log_counts(c):
                act.wait_ge(counts_bounded, 1 if isinstance(c, int) and c == 0 else 2)
                wait_if(act, inverse_ready, c)
                act.sem_inc(log_count_turn, 1)
                act.activation(log_count, norm[:, bass.ds(c * CN, CN)], ACT.Ln).then_inc(log_count_ready, 1)

            def invert_counts(c):
                act.wait_ge(log_count_ready, c + 1)
                wait_if(act, inverse_used, c)
                act.activation(inverse_count, log_count, ACT.Exp, scale=-1.0).then_inc(inverse_ready, 1)

            def exp_part(c):
                act.wait_ge(update_ready, c + 1)
                wait_if(act, softp_turned, c)
                act.activation(softp, updateT, ACT.Abs).then_inc(softp_step, 1)
                act.wait_ge(softp_step, c * 2 + 1)
                act.activation(softp, softp, ACT.Exp, scale=-1.0).then_inc(softp_step, 1)

            def log_part(c):
                act.wait_ge(softp_step, c * 2 + 2)
                act.activation(softp, softp, ACT.Ln, bias=1.0).then_inc(softp_ready, 1)

            def store_query(c):
                act.wait_ge(qk_ready, c + 1)
                act.wait_ge(stats_ready, 1)
                act.activation(QK[:, bass.ds(c * CN, CN)], two_banks(pD)[:, 0:CN], ACT.Copy,
                               scale=SCALE).then_inc(qk_stored, 1)

            def make_h2(c):
                root(var2, rstd2, c + 2)
                act.wait_ge(ln2_ready, c + 1)
                wait_if(act, h2_turned, c)
                wait_if(act, h2_stored, c * 16)
                act.sem_inc(h2_turn, 1)
                for t in range(CT):
                    a = act.activation(h2[:, t, :], X[:, bass.ds(c * CT + t, 1), :].squeeze(1), ACT.Relu,
                                       bias=shift2[:, t:t + 1], scale=rstd2[:, t:t + 1])
                a.then_inc(h2_ready, 1)

            def update_chunk(c, before=2, after=3):
                exp_part(c)
                if after >= 2:
                    invert_counts(c + 2)
                log_part(c)
                if after >= 3:
                    log_counts(c + 3)
                if before >= 2:
                    store_query(c - 2)
                if before >= 1:
                    make_h2(c - 1)

            for c in range(2):
                log_counts(c)
                invert_counts(c)
            log_counts(2)
            update_chunk(0, before=0)
            update_chunk(1, before=1)
            update_chunk(2)
            with act.Fori(3, CHUNKS - 3) as c:
                update_chunk(c)
            for after in range(2, -1, -1):
                update_chunk(CHUNKS - 1 - after, after=after)
            store_query(CHUNKS - 2)
            make_h2(CHUNKS - 1)
            store_query(CHUNKS - 1)

            TURNS = [range(0, 4), range(4, 7), range(7, 10), range(10, 13)]

            def copy_rowsT(m, n):
                for q, tiles in enumerate(TURNS):
                    act.wait_ge(rows_turned, m * 4 + q + 1)
                    if q == 0:
                        wait_if(act, scores_ready, n)
                    a, b = tiles[0], tiles[-1] + 1
                    act.activation(rowsT[:, a:b, :],
                                   pA[:, q % 2, 0:(b - a) * P].rearrange("p (j e) -> p j e", e=P),
                                   ACT.Copy).then_inc(rowsT_ready, 1)

            def exps(slot, n, lag):
                act.wait_ge(drop_ready, n + 1)
                wait_if(act, scaled, n - lag + 1)
                act.activation(rescale[:, slot], drop[:, :], ACT.Exp).then_inc(rescale_ready, 1)
                act.wait_ge(centred_ready, n + 1)
                act.activation(centred, centred, ACT.Exp).then_inc(exp_ready, 1)

            copy_rowsT(0, 0)
            for g in range(2):
                copy_rowsT(g + 1, g + 1)
                exps(g, g, 2)
            with act.Fori(1, G // 2 - 1) as k:
                for i in range(2):
                    g = k * 2 + i
                    copy_rowsT(g + 1, g + 1)
                    exps(i, g, 2)
            copy_rowsT(G - 1, G - 1)
            exps(0, G - 2, 2)
            exps(1, G - 1, 2)
            with act.If(wide > 0):
                with act.Fori(0, G) as g:
                    copy_rowsT(g + G, g * NW + WIDE)
                    with act.Fori(0, NW) as w:
                        exps(0, g * NW + w + WIDE, 1)

            def copy_sums(i, c):
                wait_if(act, out_mm, c - 1)
                act.wait_ge(all_added, 1)
                act.activation(agg_sumT[i], sums_norms[:, :, bass.ds(c * CN, CN)], ACT.Copy).then_inc(aggT_ready, 1)

            for i in range(2):
                copy_sums(i, i)
            with act.Fori(1, CHUNKS // 2) as k:
                for i in range(2):
                    copy_sums(i, k * 2 + i)

        @block.vector
        def _(dve):
            dve.wait_ge(dst_loaded, 32)
            dve.tensor_copy(dst_f[:, :], dst_i).then_inc(prep, 1)
            dve.wait_ge(prep, 1)
            by_group = dst_f[:, :].rearrange("p (g j) -> p g j", j=J)
            dve.tensor_reduce(low_p[:, :], by_group, AX.X, ALU.min).then_inc(prep, 1)
            dve.tensor_reduce(high_p[:, :], by_group, AX.X, ALU.max).then_inc(prep, 1)

            dve.wait_ge(weight_turned, 1)
            dve.tensor_copy(WnT[:, :], pA[:, 0, 0:P]).then_inc(weight_copied, 1)
            dve.tensor_copy(WeT[:, :], pA[:, 0, P:2 * P]).then_inc(weight_copied, 1)
            dve.tensor_copy(WgT[:, :], pA[0:GF, 0, 2 * P:3 * P]).then_inc(weight_copied, 1)
            dve.tensor_copy(WpT[:, :], pA[:, 0, 3 * P:4 * P]).then_inc(weight_copied, 1)
            dve.wait_ge(weight_turned, 2)
            dve.tensor_copy(Wqk[:, :], pA[:, 1, 0:P]).then_inc(weight_copied, 1)

            dve.wait_ge(bounds_turned, 1)
            dve.tensor_reduce(low[:, :], pD[0:G, 0, 0:P], AX.X, ALU.min).then_inc(prep, 1)
            dve.tensor_reduce(high[:, :], pD[0:G, 0, P:2 * P], AX.X, ALU.max).then_inc(prep, 1)
            dve.wait_ge(prep, 5)
            dve.wait_ge(const_made, 5)
            dve.tensor_scalar(low_diag[:, :], ident[0:G, 0:G], low[:, 0:1], None, ALU.mult).then_inc(prep, 1)
            dve.wait_ge(bounds_turned, 3)
            dve.tensor_copy(base_i[:, :], pD[0:1, 1, 0:G]).then_inc(prep, 1)
            dve.tensor_copy(span_row[:, :], pD[0:1, 1, 0:G]).then_inc(prep, 1)
            dve.wait_ge(prep, 8)
            dve.tensor_tensor(span_row[:, :], pD[0:1, 1, P:P + G], span_row[:, :], ALU.subtract).then_inc(prep, 1)
            dve.wait_ge(prep, 9)
            dve.tensor_reduce(widest[:, :], span_row[:, :], AX.X, ALU.max).then_inc(prep, 1)
            dve.wait_ge(prep, 10)
            dve.tensor_scalar(wide_i[:, :], widest[:, :], float(W), None, ALU.is_ge).then_inc(base_ready, 1)
            dve.wait_ge(repeated_masked, 1)
            dve.tensor_tensor(dst_w[:, :].rearrange("p (g j) -> p g j", j=J), by_group,
                              pD[:, 1, 0:G].unsqueeze(2).to_broadcast([P, G, J]), ALU.subtract).then_inc(prep, 1)
            dve.wait_ge(weight_turned, 3)
            dve.tensor_copy(Wvp[:, :], pB[:, 0, 0:P]).then_inc(weight_copied, 1)
            dve.tensor_copy(global_part[:, :], pB[:, 0, P:P + 1]).then_inc(weight_copied, 1)
            dve.wait_ge(prep, 11)
            dve.wait_ge(zeroed, 1)

            def make_onehot(hot, cols, used, ready):
                wait_if(dve, sums_ready, used)
                dve.tensor_tensor(hot, over_tiles(window_iota[:, :]), over_window(cols),
                                  ALU.is_equal).then_inc(ready, 1)

            def split_residue(slot, edge_slot, loads, used):
                dve.wait_ge(edges_loaded[edge_slot], loads)
                wait_if(dve, sums_ready, used)
                dve.tensor_tensor(residue[slot], rows[:, edge_slot], upper(rows[:, edge_slot]), ALU.subtract) \
                    .then_inc(residue_ready, 1)

            def split_rest(slot, m, used):
                dve.wait_ge(residue_ready, m + 1)
                wait_if(dve, sums_ready, used)
                dve.tensor_tensor(lowest[slot][:, POOL_TILES:J], residue[slot][:, POOL_TILES:J],
                                  upper(residue[slot])[:, POOL_TILES:J], ALU.subtract).then_inc(lowest_rest_ready, 1)

            def add_sums(slot, base, n):
                dve.wait_ge(sums_ready, n + 1)
                wait_if(dve, sums_added, n)
                a = sums_norms[:, :, bass.ds(base, W)]
                dve.tensor_tensor(a, a, pA[:, slot, 0:2 * W].rearrange("p (s n) -> p s n", n=W), ALU.add) \
                    .then_inc(sums_added, 1)

            def group_cols(t, g):
                return t[:, bass.ds(g * J, J)]

            def edge_parts(i, g, loads):
                make_onehot(onehot16[i], group_cols(dst_w, g), g - RING + 1, onehot_ready)
                split_residue(i % 2, i, loads, g - 1)

            def edge_round(k, first=False):
                for i in range(RING):
                    g = k * RING + i
                    edge_parts(i, g, (k + 1) * 16)
                    if not first or i >= 2:
                        add_sums(i % 2, load_base(dve, g - 2), g - 2)
                    split_rest(i % 2, g, g - 1)

            def newton_root(v, r, work, turn):
                dve.wait_ge(root_ready, turn)
                dve.tensor_tensor(work, r, r, ALU.mult).then_inc(newton_step, 1)
                dve.wait_ge(newton_step, turn * 4 - 3)
                dve.tensor_tensor(work, work, v, ALU.mult).then_inc(newton_step, 1)
                dve.wait_ge(newton_step, turn * 4 - 2)
                dve.tensor_scalar(work, work, -0.5, 1.5, ALU.mult, ALU.add).then_inc(newton_step, 1)
                dve.wait_ge(newton_step, turn * 4 - 1)
                dve.tensor_tensor(r, r, work, ALU.mult).then_inc(newton_step, 1)
                dve.wait_ge(newton_step, turn * 4)

            edge_round(0, first=True)
            with dve.Fori(1, NODE_START) as k:
                edge_round(k)
            dve.wait_ge(squares_ready, TILES)
            dve.tensor_scalar(var1[:, :], squares1[:, :], 1.0 / D, LN_EPS, ALU.mult, ALU.add).then_inc(var_ready, 1)
            newton_root(var1[:, :], rstd1[:, :], newton1[:, :], 1)
            dve.wait_ge(mean1_ready, 1)
            dve.tensor_tensor(shift1[:, :], negmean1[:, :], rstd1[:, :], ALU.mult).then_inc(stats_ready, 1)
            with dve.Fori(NODE_START, G // RING) as k:
                edge_round(k)
            for g in range(G - 2, G):
                add_sums(g % 2, load_base(dve, g), g)

            wide = load_wide(dve)

            def next_window(step_sem):
                dve.tensor_scalar(rel[:, :], rel[:, :], float(W), None, ALU.subtract).then_inc(step_sem, 1)

            with dve.If(wide > 0):
                dve.tensor_scalar(wide_f, dst_f[:, :], 1.0, None, ALU.add).then_inc(wide_step, 1)
                dve.wait_ge(wide_step, 1)
                dve.scalar_tensor_tensor(out=wide_f, in0=dst_w[:, :], scalar=float(W), in1=wide_f, op0=ALU.is_ge,
                                         op1=ALU.mult).then_inc(wide_step, 1)
                dve.wait_ge(wide_step, 2)
                dve.tensor_scalar(wide_f, wide_f, 1.0, None, ALU.subtract).then_inc(wide_step, 1)
                dve.wait_ge(wide_step, 3)
                with dve.Fori(0, G) as g:
                    split_residue(0, 0, (g + G // RING + 1) * 16, g * NW + WIDE)
                    split_rest(0, g + G, g * NW + WIDE)
                    dve.wait_ge(onehot_ready, g * NW + WIDE)
                    dve.tensor_copy(rel[:, :], group_cols(wide_f, g)).then_inc(wide_step, 1)
                    with dve.Fori(0, NW) as w:
                        n = g * NW + w + WIDE
                        dve.wait_ge(wide_step, g * (NW + 1) + w + 4)
                        make_onehot(onehot16[0], rel[:, :], n, onehot_ready)
                        dve.wait_ge(onehot_ready, n + 1)
                        next_window(wide_step)
                        add_sums(0, w * W, n)

            def make_update(c):
                dve.wait_ge(stats_ready, 1)
                dve.wait_ge(update_mm, c + 1)
                wait_if(dve, softp_ready, c)
                wait_if(dve, softp_summed, c)
                dve.tensor_tensor(updateT, two_banks(pB)[:, 0:CN], top[:, bass.ds(c * CN, CN)], ALU.add) \
                    .then_inc(update_ready, 1)

            def sum_softplus(c):
                dve.wait_ge(softp_ready, c + 1)
                dve.scalar_tensor_tensor(out=softp, in0=updateT, scalar=0.0, in1=softp,
                                         op0=ALU.max, op1=ALU.add).then_inc(softp_summed, 1)

            def scale_h2(c):
                wait_if(dve, h2_ready, c)
                newton_root(var2[:, :], rstd2[:, :], newton2[:, :], c + 2)
                dve.scalar_tensor_tensor(out=shift2[:, :], in0=mean2[:, :], scalar=-0.5, in1=rstd2[:, :],
                                         op0=ALU.mult, op1=ALU.mult).then_inc(ln2_ready, 1)

            def add_update(c):
                dve.wait_ge(stats_ready, 1)
                dve.wait_ge(softp_turned, c + 1)
                xc = X[:, bass.ds(c * CT, CT), :]
                dve.scalar_tensor_tensor(out=xc, in0=node_tiles(pA)[0:NT], scalar=-LN2, in1=xc,
                                         op0=ALU.add, op1=ALU.add).then_inc(x1_ready, 1)

            def statistics(c):
                dve.wait_ge(stats_ready, 1)
                dve.wait_ge(x1_ready, c + 1)
                for t in range(CT):
                    dve.bn_stats(stats2[:, t, :], X[:, bass.ds(c * CT + t, 1), :].squeeze(1)).then_inc(ln_step, 1)
                done = c * (CT + 5) + CT
                a, b = stats2[:, :, 1], stats2[:, :, 4]
                dve.wait_ge(ln_step, done)
                wait_if(dve, ln2_ready, c)
                dve.tensor_tensor(mean2[:, :], a, b, ALU.add).then_inc(ln_step, 1)
                dve.tensor_tensor(diff2[:, :], a, b, ALU.subtract).then_inc(ln_step, 1)
                dve.tensor_tensor(var2[:, :], stats2[:, :, 2], stats2[:, :, 5], ALU.add).then_inc(ln_step, 1)
                dve.wait_ge(ln_step, done + 3)
                dve.tensor_tensor(diff2[:, :], diff2[:, :], diff2[:, :], ALU.mult).then_inc(ln_step, 1)
                dve.wait_ge(ln_step, done + 4)
                dve.scalar_tensor_tensor(out=var2[:, :], in0=diff2[:, :], scalar=D / 4.0, in1=var2[:, :],
                                         op0=ALU.mult, op1=ALU.add).then_inc(ln_step, 1)
                dve.wait_ge(ln_step, done + 5)
                dve.tensor_scalar(var2[:, :], var2[:, :], 1.0 / D, LN_EPS, ALU.mult, ALU.add).then_inc(var_ready, 1)

            def copy_h2T(c):
                dve.wait_ge(h2_turned, c + 1)
                wait_if(dve, qk_ready, c)
                dve.tensor_copy(by_tile(h2T), node_tiles(pC, NT)).then_inc(h2T_ready, 1)

            def update_chunk(c, first=False, last=False):
                sum_softplus(c)
                if not first:
                    scale_h2(c - 1)
                add_update(c)
                if not last:
                    make_update(c + 1)
                statistics(c)
                if not first:
                    copy_h2T(c - 1)

            dve.wait_ge(sums_added, G)
            for first, n in ((0, CN), (CN, NPAD - CN)):
                dve.tensor_scalar(norm[:, first:first + n], norm[:, first:first + n], 1.0, None, ALU.max) \
                    .then_inc(counts_bounded, 1)
            dve.wait_ge(node_part_stored, PAIRS)
            make_update(0)
            update_chunk(0, first=True)
            update_chunk(1)
            with dve.Fori(2, CHUNKS - 1) as c:
                update_chunk(c)
            update_chunk(CHUNKS - 1, last=True)
            scale_h2(CHUNKS - 1)
            copy_h2T(CHUNKS - 1)

            dve.wait_ge(cleared, 2)

            def make_mask(slot, cols, n, lag):
                wait_if(dve, probs_ready, n - lag + 1)
                dve.tensor_tensor(onehot[:, slot], over_tiles(window_iota[:, :]), over_window(cols),
                                  ALU.is_equal).then_inc(hot_ready, 1)
                dve.wait_ge(hot_ready, n + 1)
                wait_if(dve, masked_ready, n)
                dve.tensor_scalar(unmask, onehot[:, slot], 1.0, BIG, ALU.subtract, ALU.mult) \
                    .then_inc(unmask_ready, 1)

            def mask_scores(slot, n):
                dve.wait_ge(unmask_ready, n + 1)
                dve.wait_ge(scores_ready, n + 1)
                wait_if(dve, centred_ready, n)
                dve.tensor_tensor(masked, scores_ps[slot], unmask, ALU.add).then_inc(masked_ready, 1)
                dve.wait_ge(masked_ready, n + 1)
                wait_if(dve, top_turned, n)
                dve.tensor_reduce(tile_top[:, :], masked.rearrange("p j n -> p n j"), AX.X, ALU.max) \
                    .then_inc(tile_top_ready, 1)

            def reduce_top(n):
                dve.wait_ge(top_turned, n + 1)
                wait_if(dve, top_spread, n)
                dve.tensor_reduce(group_top[:, :], turned_ps, AX.X, ALU.max).then_inc(group_top_ready, 1)

            def centre(base, n):
                dve.wait_ge(top_spread, n + 1)
                wait_if(dve, top_stored, n)
                wait_if(dve, centred_ready, n)
                window_top = top[:, bass.ds(base, W)]
                dve.tensor_tensor(new_top[:, :], window_top, spread_ps, ALU.max).then_inc(new_top_ready, 1)
                dve.wait_ge(new_top_ready, n + 1)
                wait_if(dve, rescale_ready, n)
                dve.tensor_tensor(drop[:, :], window_top, new_top[:, :], ALU.subtract).then_inc(drop_ready, 1)
                wait_if(dve, probs_ready, n)
                dve.tensor_tensor(centred, masked, over_tiles(new_top[:, :]), ALU.subtract) \
                    .then_inc(centred_ready, 1)
                dve.wait_ge(drop_ready, n + 1)
                dve.tensor_scalar(window_top, new_top[:, :], 0.0, None, ALU.add).then_inc(top_stored, 1)

            def weigh(slot, n):
                dve.wait_ge(exp_ready, n + 1)
                wait_if(dve, agg_ready, n)
                dve.scalar_tensor_tensor(out=probs, in0=centred, scalar=CLIP,
                                         in1=onehot[:, slot], op0=ALU.max, op1=ALU.mult).then_inc(probs_ready, 1)
                dve.wait_ge(probs_ready, n + 1)
                wait_if(dve, norm_added, n)
                dve.tensor_reduce(prob_sum[:, :], probs.rearrange("p j n -> p n j"), AX.X, ALU.add) \
                    .then_inc(prob_sum_ready, 1)

            def add_aggregate(slot, base, n):
                dve.wait_ge(rescale_ready, n + 1)
                wait_if(dve, norm_added, n)
                wait_if(dve, agg_added, n)
                a = sums_norms[:, :, bass.ds(base, W)]
                dve.tensor_tensor(a, a, rescale[:, slot:slot + 1].to_broadcast([P, 2, W]), ALU.mult) \
                    .then_inc(scaled, 1)
                a, s = acc[:, bass.ds(base, W)], norm[:, bass.ds(base, W)]
                dve.wait_ge(scaled, n + 1)
                dve.wait_ge(prob_sum_ready, n + 1)
                dve.tensor_tensor(s, s, prob_sum[:, :], ALU.add).then_inc(norm_added, 1)
                dve.wait_ge(agg_ready, n + 1)
                dve.tensor_tensor(a, a, agg_ps, ALU.add).then_inc(agg_added, 1)

            def edge_step(i, g, first=False, last=False):
                mask_scores(i, g)
                if not last:
                    make_mask(1 - i, group_cols(dst_w, g + 1), g + 1, 2)
                reduce_top(g)
                centre(load_base(dve, g), g)
                if not first:
                    add_aggregate(1 - i, load_base(dve, g - 1), g - 1)
                weigh(i, g)

            make_mask(0, group_cols(dst_w, 0), 0, 2)
            edge_step(0, 0, first=True)
            edge_step(1, 1)
            with dve.Fori(1, G // 2 - 1) as k:
                for i in range(2):
                    edge_step(i, k * 2 + i)
            edge_step(0, G - 2)
            edge_step(1, G - 1, last=True)
            add_aggregate(1, load_base(dve, G - 1), G - 1)
            with dve.If(wide > 0):
                with dve.Fori(0, G) as g:
                    dve.wait_ge(hot_ready, g * NW + WIDE)
                    dve.tensor_copy(rel[:, :], group_cols(wide_f, g)).then_inc(wide2_step, 1)
                    with dve.Fori(0, NW) as w:
                        n = g * NW + w + WIDE
                        dve.wait_ge(wide2_step, g * (NW + 1) + w + 1)
                        make_mask(0, rel[:, :], n, 1)
                        mask_scores(0, n)
                        next_window(wide2_step)
                        reduce_top(n)
                        centre(w * W, n)
                        weigh(0, n)
                        add_aggregate(0, w * W, n)
                dve.wait_ge(agg_added, WIDE + G * NW)
                dve.wait_ge(norm_added, WIDE + G * NW)

            def finish(slot, c, stored):
                dve.wait_ge(sum_mm, c + 1)
                dve.tensor_scalar(inverse[:, slot, :], pD[0:NT, slot, 0:CT], 1e-9, None, ALU.add) \
                    .then_inc(sum_bounded, 1)
                dve.wait_ge(sum_bounded, c + 1)
                dve.reciprocal(inverse[:, slot, :], inverse[:, slot, :]).then_inc(sum_inverted, 1)
                dve.wait_ge(sum_inverted, c + 1)
                dve.wait_ge(out_mm, c + 1)
                dve.wait_ge(bias_added, c + 1)
                wait_if(dve, out_stored[slot], stored)
                for t in range(CT):
                    dve.scalar_tensor_tensor(out=y[slot][:, t, :], in0=node_tiles((pB, pC)[slot])[0:NT, t, :],
                                             scalar=inverse[:, slot, t:t + 1], in1=h_in[slot][:, t, :],
                                             op0=ALU.mult, op1=ALU.add).then_inc(y_step, 1)
                dve.wait_ge(y_step, (c + 1) * CT)
                dve.wait_ge(all_added, 1)
                dve.scalar_tensor_tensor(out=y[slot], in0=y[slot], scalar=0.0, in1=X[:, bass.ds(c * CT, CT), :],
                                         op0=ALU.max, op1=ALU.add).then_inc(y_ready, 1)

            dve.wait_ge(agg_added, G)
            dve.wait_ge(norm_added, G)
            dve.sem_inc(all_added, 1)
            for i in range(2):
                finish(i, i, 0)
            with dve.Fori(1, CHUNKS // 2) as k:
                for i in range(2):
                    finish(i, k * 2 + i, k * 16)


_INS = ["x", "src", "dst", "edge_attr_128", "L0_gnn_global_feats", "L0_gnn_W", "L1_gnn_Wq", "L1_gnn_Wk",
        "L1_gnn_Wv", "L1_gnn_Wp", "L1_gnn_bp"]


def kernel(**inputs):
    import numpy as _np
    import concourse.bacc as _bacc
    from concourse import mybir as _mybir
    from concourse.bass_utils import run_bass_kernel_spmd as _run

    nc = _bacc.Bacc("TRN2", target_bir_lowering=False, num_devices=1)
    arrays, args = {}, []
    for name in _INS:
        a = _np.ascontiguousarray(inputs[name])
        arrays[f"in_{name}_dram"] = a
        args.append(nc.dram_tensor(f"in_{name}_dram", a.shape, _mybir.dt.from_np(a.dtype), kind="ExternalInput").ap())
    out = nc.dram_tensor("out_dram", inputs["x"].shape, F32, kind="ExternalOutput").ap()
    build(nc, *args, out)
    r = _run(nc, [arrays], core_ids=[0])
    return r.results[0]["out_dram"]
```
